# Optimizing a Trainium2 kernel written in Bass

```python
import numpy as np
import jax
import jax.numpy as jnp

def _softmax(x, axis=-1):
    return jax.nn.softmax(x, axis=axis)

def _gelu(x):
    return jax.nn.gelu(x, approximate=True)

def _silu(x):
    return jax.nn.silu(x)

def _sigmoid(x):
    return jax.nn.sigmoid(x)

def _layernorm(x, axis=-1, eps=1e-05):
    m = jnp.mean(x, axis=axis, keepdims=True)
    v = jnp.var(x, axis=axis, keepdims=True)
    return (x - m) / jnp.sqrt(v + eps)

def _scatter_add(tgt, idx, src, axis=0):
    return tgt.at[idx].add(src)

def _segment_sum(src, seg, n):
    return jax.ops.segment_sum(src, seg, n)
kernel_name = 'mk_macaron_d1_jaxref_r4_bab598'

def setup_inputs(seed: int=0):
    np.random.seed(seed)
    _w = jnp.asarray

    def _L0_attn_setup():
        import jax, jax.numpy as jnp
        import numpy as np
        import math
        HIDDEN = 512
        NUM_HEADS = 16
        HEAD_SIZE = HIDDEN // NUM_HEADS
        BATCH = 2
        SEQ = 512
        key = jax.random.key(seed)
        k_x, k_wq, k_bq, k_wo, k_bo = jax.random.split(key, 5)
        scale_in = 1.0 / math.sqrt(HIDDEN)
        return {'x': jax.random.normal(k_x, (BATCH, SEQ, HIDDEN), dtype=jnp.float32), 'Wqkv': jax.random.normal(k_wq, (HIDDEN, 3 * HIDDEN), dtype=jnp.float32) * scale_in, 'bqkv': jax.random.normal(k_bq, (3 * HIDDEN,), dtype=jnp.float32) * 0.01, 'Wo': jax.random.normal(k_wo, (HIDDEN, HIDDEN), dtype=jnp.float32) * scale_in, 'bo': jax.random.normal(k_bo, (HIDDEN,), dtype=jnp.float32) * 0.01}
    _L0_attn_in = _L0_attn_setup()

    def _L0_ffn_setup():
        import jax, jax.numpy as jnp
        import numpy as np
        B, S, D_IN, D_OUT = (4, 512, 512, 512)
        EPS = 1e-10
        key = jax.random.key(seed)
        kx, kw, kb = jax.random.split(key, 3)
        x = jax.random.normal(kx, (B, S, D_IN), dtype=jnp.float32)
        weight = jax.random.normal(kw, (D_OUT, D_IN), dtype=jnp.float32) * 0.02
        bias = jax.random.normal(kb, (D_OUT,), dtype=jnp.float32) * 0.02
        return {'x': x, 'weight': weight, 'bias': bias}
    _L0_ffn_in = _L0_ffn_setup()
    _d = {'L0_attn_x': _L0_attn_in['x'], 'L0_attn_Wqkv': _L0_attn_in['Wqkv'], 'L0_attn_bqkv': _L0_attn_in['bqkv'], 'L0_attn_Wo': _L0_attn_in['Wo'], 'L0_attn_bo': _L0_attn_in['bo'], 'L0_ffn_weight': _L0_ffn_in['weight'], 'L0_ffn_bias': _L0_ffn_in['bias']}
    _x0 = _d['L0_attn_x']
    _d['L0_attn_x'] = jax.random.normal(jax.random.fold_in(jax.random.key(seed), 1), (4, 1024, 512), dtype=_x0.dtype)
    del _x0
    return _d

def reference(L0_attn_x, L0_attn_Wqkv, L0_attn_bqkv, L0_attn_Wo, L0_attn_bo, L0_ffn_weight, L0_ffn_bias):

    def _L0_attn_ref(x, Wqkv, bqkv, Wo, bo):
        import jax, jax.numpy as jnp
        import numpy as np
        import math
        HIDDEN = 512
        NUM_HEADS = 16
        HEAD_SIZE = HIDDEN // NUM_HEADS
        BATCH = 2
        SEQ = 512
        b, s, _ = x.shape
        kqv = x @ Wqkv + bqkv
        kqv = kqv.reshape(b, s, 3, NUM_HEADS, HEAD_SIZE)
        q = kqv[:, :, 0]
        k = kqv[:, :, 1]
        v = kqv[:, :, 2]
        scores = jnp.einsum('bsnh,btnh->bnst', k, q) / math.sqrt(HEAD_SIZE)
        ones = jnp.ones_like(scores)
        scores = jnp.triu(scores) + -10000.0 * jnp.tril(ones, k=-1)
        attn = jax.nn.softmax(scores, axis=2)
        out = jnp.einsum('bnkq,bknh->bqnh', attn, v)
        out = out.reshape(b, s, NUM_HEADS * HEAD_SIZE)
        return out @ Wo + bo

    def _L0_ffn_ref(x, weight, bias):
        import jax, jax.numpy as jnp
        import numpy as np
        B, S, D_IN, D_OUT = (4, 512, 512, 512)
        EPS = 1e-10
        scale = jnp.mean(jnp.abs(weight))
        w_t = jnp.clip(jnp.round(weight / (scale + EPS)), -1.0, 1.0)
        w_ste = weight + jax.lax.stop_gradient(w_t * scale - weight)
        return jnp.einsum('bsi,oi->bso', x, w_ste) + bias
    x = L0_attn_x
    x = x + 0.5 * _L0_ffn_ref(_layernorm(x, axis=-1), L0_ffn_weight, L0_ffn_bias)
    x = x + _L0_attn_ref(_layernorm(x, axis=-1), L0_attn_Wqkv, L0_attn_bqkv, L0_attn_Wo, L0_attn_bo)
    x = x + 0.5 * _L0_ffn_ref(_layernorm(x, axis=-1), L0_ffn_weight, L0_ffn_bias)
    return x

_drawn_inputs = setup_inputs


def setup_inputs(seed=0):
    import zlib

    import numpy as np

    out = dict(_drawn_inputs(seed))
    spreads = {}
    factors = {'L0_attn_bqkv': 5.845, 'L0_attn_bo': 5.996}
    for name, (base, spread) in spreads.items():
        noise = np.random.default_rng([zlib.crc32(name.encode()), seed]).standard_normal(out[name].shape)
        drawn = base * np.exp(spread * noise) if base else spread * noise
        out[name] = jnp.asarray(drawn.astype(out[name].dtype))
    for name, factor in factors.items():
        out[name] = (out[name] * factor).astype(out[name].dtype)
    return out
```

```python
from contextlib import ExitStack

import concourse.bass as bass
from concourse import mybir

F32 = mybir.dt.float32
F32R = mybir.dt.float32r
BF16 = mybir.dt.bfloat16
ALU = mybir.AluOpType
ACT = mybir.ActivationFunctionType
AX = mybir.AxisListType.X

P = 128
B, S, D = 4, 1024, 512
HEADS, HD = 16, 32
TILES = S // P
KC = D // P
GROUPS = HEADS // 4
CW = 512
CHUNKS = S // CW
QPC = CW // P
SCALE = float(HD) ** -0.5
EPS_LN = 1e-5
EPS_FFN = 1e-10
NEG = -1e30
KQ = 3 * HD
HI, LO = 0, 1
K_, Q_ = 0, 1
W_COLUMN = {K_: D, Q_: 0}

RING = 4
STEPS = QPC + 2 * QPC


def step_of(i):
    c, kb = (0, i) if i < QPC else (1, i - QPC)
    return c, kb, max(0, P * kb - CW * c)


def diagonal(i):
    c, kb, _ = step_of(i)
    return kb >= QPC * c


def maxima(g, c):
    return [("A", g, h, QPC * c + r, kc) for h in range(4) for r in range(QPC) for kc in range(c + 1)]


def pieces(g):
    return [("P", g, K_, 0), ("P", g, Q_, 0), ("P", g, K_, 1), ("P", g, Q_, 1)]


def stage2():
    a = maxima(0, 0) + maxima(0, 1)
    out = pieces(0) + [("V", 0), ("V", 1), ("V", 2), ("V", 3)]
    v = 4
    for n, use in enumerate(a):
        out.append(use)
        if n == len(maxima(0, 0)) + 3:
            out.append(("M", 0, 0))
        if n % 12 == 11 and v < TILES:
            out.append(("V", v))
            v += 1
    return out


def filler(g, i):
    out = [("M", g, 1)] if i == 0 else []
    if g + 1 == GROUPS:
        return out
    if i < 4:
        return out + [pieces(g + 1)[i]]
    a0, a1 = maxima(g + 1, 0), maxima(g + 1, 1)
    if i in (5, 6):
        return a0[8 * (i - 5):8 * (i - 4)]
    if i == 7:
        return a1[0:4] + [("M", g + 1, 0)]
    if i > 7:
        return a1[4 + 7 * (i - 8):4 + 7 * (i - 7)]
    return out


def tiles1(s):
    return [(k, s - lag) for k, lag in (("T1", 0), ("F1", 1), ("T2", 3)) if 0 <= s - lag < TILES]


def tiles4(s):
    return [(k, s - lag) for k, lag in (("O", 0), ("T3", 2), ("F2", 3)) if 0 <= s - lag < TILES]


SLOTS = TILES + 3

USES = [u for s in range(SLOTS) for u in tiles1(s)] + stage2() \
    + [u for g in range(GROUPS) for i in range(STEPS) for u in filler(g, i)] \
    + [u for s in range(SLOTS) for u in tiles4(s)]
USE = {u: n for n, u in enumerate(USES)}
R = len(USES)
SETUP_USES = 6
SPLIT = {u: n for n, u in enumerate([u for u in USES if u[0] in ("T1", "T2", "T3", "P", "M")])}
NSPLIT = len(SPLIT)
assert R == len(USE) and R % RING == 0

WCHUNKS = [("QK", g, j) for g in (1, 2, 3) for j in (K_, Q_)] + [("WO", g) for g in range(KC)] \
    + [("WV", k) for k in range(KC)] + [("QK", 0, K_), ("QK", 0, Q_)]
W = len(WCHUNKS)
FIRST_W = KC + 2
WAT = {w: FIRST_W + n for n, w in enumerate(WCHUNKS)}
NS = 4 * STEPS * GROUPS
NSTEP = STEPS * GROUPS
NDIAG = 2 * QPC * GROUPS
NCH = CHUNKS * GROUPS


def macaron_kernel(nc, x, wqkv, bqkv, wo, bo, wf, bf, out):
    with ExitStack() as ctx:
        def sb(name, shape, dt=F32):
            return ctx.enter_context(nc.sbuf_tensor(name, shape, dt))

        def sem(name):
            return ctx.enter_context(nc.semaphore(name))

        xt = sb("xt", [P, TILES, D])
        wfT = sb("wfT", [P, KC, D], F32R)
        wqk = sb("wqk", [P, 2, 2, KC, P], F32R)
        stage = sb("stage", [P, 2, D])
        hT = sb("hT", [P, 2, KC, S], F32R)
        hts = sb("hts", [P, 2, 2, KC, P], F32R)
        hn = sb("hn", [P, 2, D])
        v = sb("v", [P, TILES, D])
        nat = sb("nat", [P, 2, 2, CW], F32R)
        kst = [sb(f"kst{n}", [P, CHUNKS, 4, CW], F32R) for n in range(2)]
        qst = [sb(f"qst{n}", [P, CHUNKS, 4, CW], F32R) for n in range(2)]
        prob = sb("prob", [P, 2, 4, CW])
        o32 = sb("o32", [P, 4, CW])
        rec = sb("rec", [P, CW])
        junk = sb("junk", [P, 2, CW], BF16)
        mask = sb("mask", [P, CW], BF16)
        ident = sb("ident", [P, P])
        ones = sb("ones", [P, P])
        hb = sb("hb", [P, D])
        bo2 = sb("bo2", [P, D])
        bqk = sb("bqk", [P, 3 * KC])
        small = sb("small", [P, 8])
        st6 = sb("st6", [P, 3, 2, 6])
        mv = sb("mv", [P, 3, TILES, 2])
        ve = sb("ve", [P, 3, TILES])
        rstd = sb("rstd", [P, 3, TILES])
        nmr = sb("nmr", [P, 3, TILES])
        mst = sb("mst", [P, 3, 4 * QPC])
        mcol = sb("mcol", [P, 4 * QPC])
        mrow = sb("mrow", [4 * QPC, 2, 2, P], F32R)
        scr = nc.dram_tensor("stack_scratch", [2, CHUNKS, 2, HD, 4, CW], F32, kind="Internal").ap()

        wvT, woT = qst[1], qst[0]
        bank = [ctx.enter_context(nc.psum_tensor(f"bank{n}", [P, CW], F32)) for n in range(8)]
        sbank, accv, accs = bank[4:6], bank[6], bank[7]

        ring_full, ring_free = sem("ring_full"), sem("ring_free")
        hi_done = sem("hi_done")
        s_full, s_exp = sem("s_full"), sem("s_exp")
        masked, step_used = sem("masked"), sem("step_used")
        acc_free, rec_done = sem("acc_free"), sem("rec_done")
        o_hi, o_split = sem("o_hi"), sem("o_split")
        w_hi, w_split = sem("w_hi"), sem("w_split")
        st_done = [sem(f"st_done{n}") for n in range(3)]
        mv_done = [sem(f"mv_done{n}") for n in range(3)]
        ve_done = [sem(f"ve_done{n}") for n in range(3)]
        rs_done = [sem(f"rs_done{n}") for n in range(3)]
        nm_done = [sem(f"nm_done{n}") for n in range(3)]
        hn_done = [sem(f"hn_done{n}") for n in range(3)]
        xb_done = [sem(f"xb_done{n}") for n in range(3)]
        mcol_done = sem("mcol_done")
        x_in = [sem(f"x_in{t}") for t in range(TILES)]
        x_out = [sem(f"x_out{t}") for t in range(TILES)]
        staged = [sem(f"staged{n}") for n in range(2)]
        scr_in = sem("scr_in")
        stk_in = [[sem(f"stk_in{j}{c}") for c in range(CHUNKS)] for j in range(2)]
        mrow_in = [sem(f"mrow_in{c}") for c in range(CHUNKS)]
        set_wf, set_wo, set_b = sem("set_wf"), sem("set_wo"), sem("set_b")
        set_pool, set_dve = sem("set_pool"), sem("set_dve")

        def used(b, u):
            return b * R + (SETUP_USES + USE[u] + 1)

        def split(b, u):
            return b * NSPLIT + (SPLIT[u] + 1)

        def ring(u):
            return bank[(SETUP_USES + USE[u]) % RING][:, :]

        def tile(b, t):
            return b * TILES + (t + 1)

        def exps(b, n):
            return b * NS + (n + 3)

        def stepped(b, n):
            return b * NSTEP + (n + 3)

        def chunked(b, n):
            return b * NCH + (n + 2)

        def out_split(b, n):
            return b * NCH + (n + 5)

        def wsplit(b, w):
            return b * W + (WAT[w] + 1)

        def group(b, g, per):
            return b * (GROUPS * per) + per * (g + 1)

        def source(w):
            if w[0] == "QK":
                at = W_COLUMN[w[2]] + P * w[1]
                return wqkv[:, at:at + P].rearrange("(k p) n -> p k n", p=P)
            if w[0] == "WO":
                return wo[P * w[1]:P * w[1] + P, :]
            return wqkv[P * w[1]:P * w[1] + P, 2 * D:3 * D]

        def target(w, part):
            if w[0] == "QK":
                return wqk[:, part, w[2], :, :].rearrange("p k n -> p (k n)")
            return (woT if w[0] == "WO" else wvT)[:, part, w[1], :]

        def stage_as(w, n):
            return stage[:, n, :].rearrange("p (k n) -> p k n", k=KC) if w[0] == "QK" else stage[:, n, :]

        def blocks(u):
            return ring(u).rearrange("p (k n) -> p k n", k=KC)

        def bias_of(j, g):
            return bqk[:, KC * (j == K_) + g:KC * (j == K_) + g + 1]

        dve_past, pool_past, sp_past = sem("dve_past"), sem("pool_past"), sem("sp_past")
        block = ctx.enter_context(nc.Block())

        @block.sync
        def _(sp):
            sp.dma_start(prob[:, 0, :, :], wf.rearrange("(k p) n -> p k n", p=P)).then_inc(set_wf, 16)
            sp.dma_start(xt[:, 0, :], x[0, 0:P, :]).then_inc(x_in[0], 16)
            sp.dma_start(hb[:, :], bf.partition_broadcast(P)).then_inc(set_b, 16)
            sp.dma_start(bo2[:, :], bo.partition_broadcast(P)).then_inc(set_b, 16)
            sp.dma_start(bqk[:, :], bqkv.rearrange("(k p) -> p k", p=P), allow_slow_non_contiguous=True).then_inc(set_b, 16)
            sp.dma_start(v[:, 0:KC, :], wo.rearrange("(k p) n -> p k n", p=P)).then_inc(set_wo, 16)
            for t in range(1, TILES):
                sp.dma_start(xt[:, t, :], x[0, P * t:P * t + P, :]).then_inc(x_in[t], 16)
            for n, w in enumerate(WCHUNKS[-FIRST_W:]):
                if n >= 2:
                    sp.wait_ge(w_split, n - 1)
                sp.dma_start(stage_as(w, n % 2), source(w)).then_inc(staged[n % 2], 16)

            def load_weights(b, w):
                n = WAT[w]
                sp.wait_ge(w_split, b * W + (n - 1))
                sp.dma_start(stage_as(w, n % 2), source(w)).then_inc(staged[n % 2], 16)

            def stack(b, g, j, c, first_free):
                u = ("P", g, j, c)
                lay = scr[j, c]
                if first_free is not None:
                    sp.wait_ge(s_full, first_free)
                    sp.sem_inc(sp_past, 1)
                sp.wait_ge(hi_done, split(b, u))
                sp.dma_start(lay[HI].rearrange("r h n -> h r n"), nat[:, j, HI, :].bitcast(F32)).then_inc(scr_in, 16)
                sp.wait_ge(ring_free, used(b, u))
                sp.dma_start(lay[LO].rearrange("r h n -> h r n"), nat[:, j, LO, :].bitcast(F32)).then_inc(scr_in, 16)
                n = pieces(g).index(u)
                sp.wait_ge(scr_in, b * (GROUPS * 128) + (128 * g + 32 * (n + 1)))
                both = lay.rearrange("l r h n -> (l r) h n")
                dst = (kst, qst)[j][g % 2]
                pair, single = ((0, 2 * HD), (2 * HD, KQ)) if j == K_ else ((HD, KQ), (0, HD))
                sp.dma_start(dst[pair[0]:pair[1], c, :, :].bitcast(F32), both).then_inc(stk_in[j][c], 16)
                sp.dma_start(dst[single[0]:single[1], c, :, :].bitcast(F32), both[0:HD]).then_inc(stk_in[j][c], 16)

            def rows(b, g, c):
                sp.wait_ge(ring_free, used(b, ("M", g, c)))
                for part in (HI, LO):
                    row = KQ + part
                    sp.dma_start(qst[g % 2][row:row + 1, c, :, :].rearrange("p h n -> p (h n)").bitcast(F32),
                                 mrow[:, c, part, :].bitcast(F32)).then_inc(mrow_in[c], 16)

            def event(b, u):
                if u[0] == "P":
                    g = u[1]
                    stack(b, *u[1:], b * NS + 4 * STEPS * (g - 1) if g >= 2 else None)
                if u[0] == "M":
                    rows(b, *u[1:])

            def sequence(b, more):
                load_weights(b, ("QK", 1, K_))
                load_weights(b, ("QK", 1, Q_))
                for u in stage2():
                    event(b, u)
                load_weights(b, ("QK", 2, K_))
                load_weights(b, ("QK", 2, Q_))
                for g in range(GROUPS):
                    for i in range(STEPS):
                        for u in filler(g, i):
                            event(b, u)
                        if i == 7:
                            if g == 0:
                                load_weights(b, ("QK", 3, K_))
                                load_weights(b, ("QK", 3, Q_))
                            if g == 1:
                                load_weights(b, ("WO", 0))
                                load_weights(b, ("WO", 1))
                load_weights(b, ("WO", 2))
                load_weights(b, ("WO", 3))
                load_weights(b, ("WV", 0))
                load_weights(b, ("WV", 1))
                for t in range(TILES + 1):
                    if t < TILES:
                        if t < FIRST_W - 2:
                            load_weights(b, WCHUNKS[W - FIRST_W + 2 + t])
                        sp.wait_ge(ring_free, used(b, ("F2", t)))
                        sp.sem_inc(sp_past, 1)
                        sp.dma_start(out[b, P * t:P * t + P, :], xt[:, t, :]).then_inc(x_out[t], 16)
                    if more and t > 0:
                        sp.wait_ge(x_out[t - 1], b * 16 + 16)
                        sp.sem_inc(sp_past, 1)
                        sp.dma_start(xt[:, t - 1, :], x[b + 1, P * (t - 1):P * t, :]).then_inc(x_in[t - 1], 16)

            with sp.Fori(0, B - 1) as b:
                sequence(b, True)
            sequence(B - 1, False)
            for t in range(TILES):
                sp.wait_ge(x_out[t], 16 * B)

        @block.gpsimd
        def _(pool):
            nc.gpsimd.memset(ident[:, :], 0.0).then_inc(set_pool, 1)
            nc.gpsimd.memset(mask[:, :], 0.0).then_inc(set_pool, 1)
            nc.gpsimd.memset(ones[:, :], 1.0).then_inc(set_pool, 1)
            nc.gpsimd.memset(small[:, 4:5], -0.5).then_inc(set_pool, 1)
            pool.wait_ge(set_pool, 4)
            nc.gpsimd.affine_select(out=ident[:, :], in_=ident[:, :], compare_op=ALU.not_equal, fill=1.0, base=0,
                                    pattern=[[-1, P]], channel_multiplier=1).then_inc(set_pool, 1)
            nc.gpsimd.affine_select(out=mask[:, CW - P:CW], in_=mask[:, CW - P:CW], compare_op=ALU.is_ge, fill=NEG,
                                    base=0, pattern=[[-1, P]], channel_multiplier=1).then_inc(set_pool, 1)
            pool.wait_ge(set_pool, 6)
            pool.wait_ge(set_b, 48)
            nc.gpsimd.tensor_scalar(hb[:, :], hb[:, :], 0.5, 0.0, ALU.mult, ALU.add).then_inc(o_split, 4)
            pool.wait_ge(o_split, 4)

            def split_chunk(w, n, slot, base):
                pool.wait_ge(staged[slot], n * 16)
                pool.sem_inc(pool_past, 1)
                nc.gpsimd.tensor_copy(target(w, HI), stage[:, slot, :]).then_inc(w_hi, 1)
                pool.wait_ge(w_hi, base)
                nc.gpsimd.tensor_tensor(target(w, LO), stage[:, slot, :], target(w, HI).bitcast(F32), ALU.subtract)\
                    .then_inc(w_split, 1)

            for n, w in enumerate(WCHUNKS[-FIRST_W:]):
                split_chunk(w, n // 2 + 1, n % 2, n + 1)

            def weights(b, w):
                n = WAT[w]
                split_chunk(w, b * (W // 2) + (n // 2 + 1), n % 2, wsplit(b, w))

            def rsqrt(b, l, t):
                pool.wait_ge(mv_done[l], tile(b, t))
                pool.sem_inc(pool_past, 1)
                nc.gpsimd.tensor_scalar(ve[:, l, t:t + 1], mv[:, l, t, 1:2], 1.0, EPS_LN, ALU.mult, ALU.add)\
                    .then_inc(ve_done[l], 1)
                pool.wait_ge(ve_done[l], tile(b, t))
                nc.gpsimd.tensor_tensor(rstd[:, l, t:t + 1], ve[:, l, t:t + 1], small[:, 4:5], ALU.pow)\
                    .then_inc(rs_done[l], 1)

            def add_bias(b, l, t):
                pool.wait_ge(hn_done[l], tile(b, t))
                nc.gpsimd.tensor_tensor(xt[:, t, :], xt[:, t, :], (bo2 if l == 1 else hb)[:, :], ALU.add)\
                    .then_inc(xb_done[l], 1)

            def split_output(b, n):
                g, c = n // CHUNKS, n % CHUNKS
                pool.wait_ge(acc_free, chunked(b, n))
                hi, lo = (hT[:, part, g, CW * c:CW * c + CW] for part in (HI, LO))
                pool.sem_inc(pool_past, 1)
                nc.gpsimd.tensor_copy(hi, o32[:, n % 4, :]).then_inc(o_hi, 1)
                pool.wait_ge(o_hi, b * NCH + (n + 1))
                nc.gpsimd.tensor_tensor(lo, o32[:, n % 4, :], hi.bitcast(F32), ALU.subtract).then_inc(o_split, 1)

            def step(b, g, i):
                if diagonal(i):
                    n = STEPS * g + i
                    off = step_of(i)[2]
                    pool.wait_ge(s_exp, exps(b, 4 * n + 3))
                    part = prob[:, n % 2, :, off:off + P]
                    pool.sem_inc(pool_past, 1)
                    nc.gpsimd.affine_select(out=part, in_=part, compare_op=ALU.is_ge, fill=0.0, base=0,
                                            pattern=[[0, 4], [1, P]], channel_multiplier=-1).then_inc(masked, 1)

            with pool.Fori(0, B) as b:
                rsqrt(b, 0, 0)
                for s in range(SLOTS):
                    if s + 1 < TILES:
                        rsqrt(b, 0, s + 1)
                    if s < TILES:
                        add_bias(b, 0, s)
                    if 0 <= s - 1 < TILES:
                        rsqrt(b, 1, s - 1)
                    if 0 <= s - 2 < TILES:
                        add_bias(b, 1, s - 2)
                pool.wait_ge(ring_full, used(b, pieces(0)[-1]))
                weights(b, ("QK", 1, K_))
                weights(b, ("QK", 1, Q_))
                for g in range(GROUPS):
                    for i in range(STEPS):
                        step(b, g, i)
                        if i == 3 and g < 2:
                            pool.wait_ge(ring_full, used(b, pieces(g + 1)[-1]))
                            weights(b, ("QK", g + 2, K_))
                            weights(b, ("QK", g + 2, Q_))
                        if i == 3 and g == 2:
                            pool.wait_ge(ring_full, used(b, pieces(3)[-1]))
                            for n in range(4):
                                split_output(b, n)
                        if i == 5 and g == 2:
                            split_output(b, 4)
                        if i == 4 and g == 3:
                            split_output(b, 5)
                            pool.wait_ge(s_full, b * NS + 3 * 4 * STEPS)
                            weights(b, ("WO", 0))
                        if i == 5 and g == 3:
                            split_output(b, 6)
                        if 5 <= i < 8 and g == 3:
                            weights(b, ("WO", i - 4))
                split_output(b, 7)
                pool.wait_ge(s_full, b * NS + NS)
                for s in range(SLOTS):
                    if s < TILES:
                        rsqrt(b, 2, s)
                    if 0 <= s - 2 < TILES:
                        add_bias(b, 2, s - 2)
                    if s < FIRST_W:
                        weights(b, WCHUNKS[W - FIRST_W + s])

        @block.vector
        def _(dve):
            def filled(n):
                return dve.wait_ge(ring_full, n)

            wn, wt = prob[:, 0, :, :], prob[:, 1, :, :]
            dve.wait_ge(set_wf, 16)
            nc.vector.tensor_reduce(small[:, 0:1], wn.rearrange("p k n -> p (k n)"), AX, ALU.add,
                                    apply_absolute_value=True).then_inc(set_dve, 1)
            filled(1)
            nc.vector.tensor_scalar(small[:, 1:2], bank[0][:, 0:1], 1.0 / (D * D), None, ALU.mult).then_inc(ring_free, 1)
            dve.wait_ge(ring_free, 1)
            nc.vector.tensor_scalar(small[:, 2:3], small[:, 1:2], EPS_FFN, 0.5, ALU.add, ALU.mult).then_inc(set_dve, 1)
            nc.vector.tensor_scalar(small[:, 5:6], small[:, 1:2], 0.5, None, ALU.mult).then_inc(set_dve, 1)
            dve.wait_ge(set_dve, 3)
            nc.vector.tensor_scalar(small[:, 3:4], small[:, 2:3], -1.0, None, ALU.mult).then_inc(set_dve, 1)
            dve.wait_ge(set_dve, 4)
            flat = [a.rearrange("p k n -> p (k n)") for a in (wn, wt)]
            nc.vector.tensor_scalar(flat[1], flat[0], small[:, 3:4], None, ALU.is_lt).then_inc(set_dve, 1)
            dve.wait_ge(set_dve, 5)
            nc.vector.scalar_tensor_tensor(flat[1], flat[0], small[:, 2:3], flat[1], ALU.is_gt, ALU.subtract)\
                .then_inc(set_dve, 1)
            dve.wait_ge(set_b, 48)
            dve.wait_ge(set_pool, 6)
            for k in range(KC):
                nc.vector.tensor_scalar(o32[:, 0, P * k:P * k + P], ones[:, :], bqk[:, 2 * KC + k:2 * KC + k + 1], None,
                                        ALU.mult).then_inc(set_dve, 1)
            for n in range(2):
                nc.vector.memset(kst[n][KQ:KQ + 2, :, :, :].bitcast(F32), 1.0).then_inc(set_dve, 1)
            nc.vector.memset(rec[:, :], 0.0).then_inc(acc_free, 1)
            dve.wait_ge(acc_free, 1)
            for k in range(KC):
                filled(2 + k)
                nc.vector.tensor_copy(wfT[:, k, :], bank[(1 + k) % RING][:, :]).then_inc(ring_free, 1)
            filled(6)
            nc.vector.tensor_tensor(bo2[:, :], bank[5 % RING][:, :], bo2[:, :], ALU.add).then_inc(ring_free, 1)

            def stats(b, l, t):
                if l == 0:
                    dve.wait_ge(x_in[t], b * 16 + 16)
                else:
                    dve.wait_ge(ring_free, used(b, (("F1", "O")[l - 1], t)))
                s = st6[:, l, t % 2, :]
                nc.vector.bn_stats(s, xt[:, t, :]).then_inc(st_done[l], 1)
                dve.wait_ge(st_done[l], tile(b, t))
                dve.sem_inc(dve_past, 1)
                nc.vector.bn_aggr(mv[:, l, t, :], s).then_inc(mv_done[l], 1)

            def shift(b, l, t):
                dve.wait_ge(rs_done[l], tile(b, t))
                nc.vector.scalar_tensor_tensor(nmr[:, l, t:t + 1], mv[:, l, t, 0:1], -1.0, rstd[:, l, t:t + 1],
                                               ALU.mult, ALU.mult).then_inc(nm_done[l], 1)

            def low(b, u, dst, src, hi, first=None):
                dve.wait_ge(hi_done, split(b, u))
                if first is None:
                    i = nc.vector.tensor_tensor(dst, src, hi.bitcast(F32), ALU.subtract)
                else:
                    i = nc.vector.scalar_tensor_tensor(dst, src, first[0], hi.bitcast(F32), first[1], ALU.subtract)
                i.then_inc(ring_free, 1)

            def residual(b, u, l):
                t = u[1]
                dve.wait_ge(ring_full, used(b, u))
                dve.wait_ge(xb_done[l], tile(b, t))
                if l == 1:
                    nc.vector.tensor_tensor(xt[:, t, :], ring(u)[:, :], xt[:, t, :], ALU.add).then_inc(ring_free, 1)
                else:
                    nc.vector.scalar_tensor_tensor(xt[:, t, :], ring(u)[:, :], small[:, 5:6], xt[:, t, :],
                                                   ALU.mult, ALU.add).then_inc(ring_free, 1)

            def maximum(b, u):
                _, g, h, qb, kc = u
                c, r = qb // QPC, qb % QPC
                dve.wait_ge(ring_full, used(b, u))
                at = 4 * h + r
                if kc < c:
                    nc.vector.tensor_reduce(mst[:, 1, at:at + 1], ring(u)[:, :], AX, ALU.max).then_inc(ring_free, 1)
                else:
                    n = P * (r + 1)
                    dve.wait_ge(ring_free, used(b, u) - 2)
                    dve.sem_inc(dve_past, 1)
                    nc.vector.tensor_tensor_reduce(junk[:, USE[u] % 2, 0:n], ring(u)[:, 0:n], mask[:, CW - n:CW], 1.0,
                                                   -3e38, ALU.add, ALU.max, mst[:, 2 * c, at:at + 1])\
                        .then_inc(ring_free, 1)
                if u == maxima(g, 1)[-1]:
                    dve.wait_ge(ring_free, used(b, u))
                    nc.vector.tensor_tensor(mcol[:, :], mst[:, 1, :], mst[:, 2, :], ALU.max).then_inc(mcol_done, 1)

            def normalise(b, n):
                dve.wait_ge(step_used, stepped(b, n // 2 * STEPS + (QPC - 1, STEPS - 1)[n % 2]))
                dve.wait_ge(acc_free, chunked(b, n - 1))
                nc.vector.reciprocal(rec[:, :], accs[:, :]).then_inc(rec_done, 1)
                dve.wait_ge(rec_done, b * NCH + (n + 1))
                dve.wait_ge(o_split, out_split(b, n - 4))
                nc.vector.tensor_tensor(o32[:, n % 4, :], accv[:, :], rec[:, :], ALU.mult).then_inc(acc_free, 1)

            def use(b, u):
                if u[0] == "A":
                    maximum(b, u)
                elif u[0] == "V":
                    dve.wait_ge(ring_full, used(b, u))
                    nc.vector.tensor_copy(v[:, u[1], :], ring(u)[:, :]).then_inc(ring_free, 1)
                elif u[0] == "P":
                    _, g, j, c = u
                    low(b, u, nat[:, j, LO, :], ring(u)[:, :], nat[:, j, HI, :], (bias_of(j, g), ALU.add))
                elif u[0] == "M":
                    c = u[2]
                    low(b, u, mrow[:, c, LO, :], ring(u)[0:4 * QPC, 0:P], mrow[:, c, HI, :], (-1.0, ALU.mult))
                elif u[0] == "T2":
                    at = slice(P * u[1], P * u[1] + P)
                    low(b, u, hT[:, LO, :, at], blocks(u), hT[:, HI, :, at])
                elif u[0] in ("T1", "T3"):
                    low(b, u, hts[:, u[1] % 2, LO, :, :], blocks(u), hts[:, u[1] % 2, HI, :, :])
                else:
                    residual(b, u, {"F1": 0, "O": 1, "F2": 2}[u[0]])

            with dve.Fori(0, B) as b:
                stats(b, 0, 0)
                stats(b, 0, 1)
                shift(b, 0, 0)
                for s in range(SLOTS):
                    for u in tiles1(s):
                        use(b, u)
                        if u[0] == "T1":
                            if s + 2 < TILES:
                                stats(b, 0, s + 2)
                            if s + 1 < TILES:
                                shift(b, 0, s + 1)
                        if u[0] == "F1":
                            stats(b, 1, s - 1)
                    if 0 <= s - 1 < TILES:
                        shift(b, 1, s - 1)
                for u in stage2():
                    use(b, u)
                for n in range(NSTEP):
                    g, i = n // STEPS, n % STEPS
                    if n and i == 0:
                        normalise(b, 2 * g - 1)
                    if i == QPC:
                        normalise(b, 2 * g)
                    for u in filler(g, i):
                        use(b, u)
                normalise(b, NCH - 1)
                for s in range(SLOTS):
                    for u in tiles4(s):
                        use(b, u)
                        if u[0] == "O":
                            stats(b, 2, s)
                    if s < TILES:
                        shift(b, 2, s)

        @block.scalar
        def _(act):
            act.wait_ge(set_pool, 6)
            nc.scalar.activation(small[:, 6:7], ones[:, 0:1], ACT.Exp).then_inc(s_exp, 2)
            act.wait_ge(set_b, 48)

            def normal(b, l, t):
                act.wait_ge(nm_done[l], tile(b, t))
                slot = (0, 1, t % 2)[l]
                nc.scalar.activation(hn[:, slot, :], xt[:, t, :], ACT.Identity, bias=nmr[:, l, t:t + 1],
                                     scale=rstd[:, l, t:t + 1]).then_inc(hn_done[l], 1)

            def high(b, u):
                kind = u[0]
                act.wait_ge(ring_full, used(b, u))
                if kind == "P":
                    _, g, j, c = u
                    n = pieces(g).index(u)
                    if g or n >= 2:
                        act.wait_ge(scr_in, b * (GROUPS * 128) + (128 * g + 32 * (n - 1)))
                    i = nc.scalar.activation(nat[:, j, HI, :], ring(u)[:, :], ACT.Identity, bias=bias_of(j, g))
                elif kind == "M":
                    i = nc.scalar.activation(mrow[:, u[2], HI, :], ring(u)[0:4 * QPC, 0:P], ACT.Identity, scale=-1.0)
                elif kind == "T2":
                    i = nc.scalar.activation(hT[:, HI, :, P * u[1]:P * u[1] + P], blocks(u), ACT.Identity)
                else:
                    i = nc.scalar.activation(hts[:, u[1] % 2, HI, :, :], blocks(u), ACT.Identity)
                i.then_inc(hi_done, 1)

            with act.Fori(0, B) as b:
                normal(b, 0, 0)
                for s in range(SLOTS):
                    if s < TILES:
                        high(b, ("T1", s))
                    if s + 1 < TILES:
                        normal(b, 0, s + 1)
                    if 0 <= s - 3 < TILES:
                        high(b, ("T2", s - 3))
                    if 0 <= s - 2 < TILES:
                        normal(b, 1, s - 2)
                for u in stage2():
                    if u in SPLIT:
                        high(b, u)
                for n in range(NSTEP):
                    g, i = n // STEPS, n % STEPS
                    off = step_of(i)[2]
                    act.wait_ge(step_used, stepped(b, n - 2))
                    for h in range(4):
                        act.wait_ge(s_full, b * NS + (4 * n + h + 1))
                        nc.scalar.activation(prob[:, n % 2, h, off:CW], sbank[h % 2][:, off:CW], ACT.Exp, scale=SCALE)\
                            .then_inc(s_exp, 1)
                    for u in filler(g, i):
                        if u in SPLIT:
                            high(b, u)
                for s in range(SLOTS):
                    if 0 <= s - 2 < TILES:
                        high(b, ("T3", s - 2))
                    if 0 <= s - 1 < TILES:
                        normal(b, 2, s - 1)

        @block.tensor
        def _(pe):
            pe.wait_ge(set_pool, 6)
            pe.wait_ge(set_dve, 1)
            nc.tensor.matmul(bank[0][:, 0:1], ones[:, :], small[:, 0:1], start=True, stop=True).then_inc(ring_full, 1)
            pe.wait_ge(set_dve, 6)
            for k in range(KC):
                if k == KC - 1:
                    pe.wait_ge(ring_free, 1)
                for o in range(KC):
                    t = nc.tensor.transpose(bank[(1 + k) % RING][:, P * o:P * o + P], prob[:, 1, o, P * k:P * k + P],
                                            ident[:, :])
                t.then_inc(ring_full, 1)
            pe.wait_ge(set_dve, 6 + KC)
            pe.wait_ge(set_wo, 16)
            pe.wait_ge(ring_free, 2)
            for k in range(KC):
                m = nc.tensor.matmul(bank[5 % RING][:, :], o32[:, 0, P * k:P * k + P], v[:, k, :], start=(k == 0),
                                     stop=(k == KC - 1))
                if k == 0:
                    m.then_inc(step_used, 2)
            m.then_inc(ring_full, 1)

            def products(b, u, left, right):
                terms = [(k, x, y) for k in range(KC) for x, y in ((HI, HI), (LO, HI), (HI, LO))]
                for n, (k, x, y) in enumerate(terms):
                    m = nc.tensor.matmul(ring(u)[:, :], left(x, k), right(y, k), start=(n == 0),
                                         stop=(n == len(terms) - 1))
                m.then_inc(ring_full, 1)

            def use(b, u):
                kind = u[0]
                pe.wait_ge(ring_free, used(b, u) - RING)
                if kind in ("T1", "T2", "T3"):
                    l, t = int(kind[1]) - 1, u[1]
                    pe.wait_ge(hn_done[l], tile(b, t))
                    for k in range(KC):
                        m = nc.tensor.transpose(ring(u)[:, P * k:P * k + P], hn[:, (0, 1, t % 2)[l], P * k:P * k + P],
                                                ident[:, :])
                    m.then_inc(ring_full, 1)
                elif kind in ("F1", "F2"):
                    t = u[1]
                    pe.wait_ge(ring_free, used(b, ("T" + ("1" if kind == "F1" else "3"), t)))
                    for k in range(KC):
                        for part in (HI, LO):
                            m = nc.tensor.matmul(ring(u)[:, :], hts[:, t % 2, part, k, :], wfT[:, k, :],
                                                 start=(k == 0 and part == HI), stop=(k == KC - 1 and part == LO))
                    m.then_inc(ring_full, 1)
                elif kind == "V":
                    t = u[1]
                    products(b, u, lambda x, k: hT[:, x, k, P * t:P * t + P], lambda y, k: wvT[:, y, k, :])
                elif kind == "P":
                    _, g, j, c = u
                    if g == 0:
                        pe.wait_ge(ring_free, used(b, ("T2", QPC * c + QPC - 1)))
                        pe.wait_ge(w_split, b * W + FIRST_W)
                    else:
                        pe.wait_ge(w_split, wsplit(b, ("QK", g, j)))
                    products(b, u, lambda x, k: wqk[:, x, j, k, :], lambda y, k: hT[:, y, k, CW * c:CW * c + CW])
                elif kind == "A":
                    _, g, h, qb, kc = u
                    c, r = qb // QPC, qb % QPC
                    if h == 0 and r == 0 and kc == 0:
                        pe.wait_ge(stk_in[K_][c], group(b, g, 32))
                        pe.wait_ge(stk_in[Q_][c], group(b, g, 32))
                    n = CW if kc < c else max(2 * P, P * (r + 1))
                    nc.tensor.matmul(ring(u)[:, 0:n], qst[g % 2][0:KQ, c, h, P * r:P * r + P],
                                     kst[g % 2][0:KQ, kc, h, 0:n], start=True, stop=True).then_inc(ring_full, 1)
                elif kind == "M":
                    _, g, c = u
                    if c == 0:
                        pe.wait_ge(ring_free, used(b, maxima(g, 0)[-1]))
                    else:
                        pe.wait_ge(mcol_done, b * GROUPS + (g + 1))
                    nc.tensor.transpose(ring(u)[0:4 * QPC, 0:P], mst[:, 0, :] if c == 0 else mcol[:, :], ident[:, :])\
                        .then_inc(ring_full, 1)
                else:
                    t = u[1]
                    pe.wait_ge(w_split, wsplit(b, ("WO", KC - 1)))
                    pe.wait_ge(o_split, out_split(b, NCH - 2 + t // QPC))
                    products(b, u, lambda x, k: hT[:, x, k, P * t:P * t + P], lambda y, k: woT[:, y, k, :])

            def scores(b, n, h):
                g, i = n // STEPS, n % STEPS
                c, kb, off = step_of(i)
                off = min(off, 2 * P)
                if h == 0 and kb == 0:
                    pe.wait_ge(mrow_in[c], group(b, g, 32))
                pe.wait_ge(s_exp, exps(b, 4 * n + h - 2))
                nc.tensor.matmul(sbank[h % 2][:, off:CW], kst[g % 2][0:KQ + 2, kb // QPC, h, P * (kb % QPC):P * (kb % QPC) + P],
                                 qst[g % 2][0:KQ + 2, c, h, off:CW], start=True, stop=True).then_inc(s_full, 1)

            def attend(b, n):
                g, i = n // STEPS, n % STEPS
                c, kb, off = step_of(i)
                if kb == 0:
                    pe.wait_ge(acc_free, chunked(b, 2 * g + c - 1))
                if n == 0:
                    pe.wait_ge(ring_free, used(b, ("V", TILES - 1)))
                if diagonal(i):
                    pe.wait_ge(masked, b * NDIAG + (2 * QPC * g + i % QPC + (QPC if c else 0) + 1))
                else:
                    pe.wait_ge(s_exp, exps(b, 4 * n + 3))
                first, last = kb == 0, kb == QPC * (c + 1) - 1
                for acc, values in ((accv, True), (accs, False)):
                    for h in range(4):
                        left = v[:, kb, P * g + HD * h:P * g + HD * h + HD] if values else ones[:, 0:HD]
                        m = nc.tensor.matmul(acc[HD * h:HD * h + HD, off:CW], left, prob[:, n % 2, h, off:CW],
                                             start=first, stop=last)
                m.then_inc(step_used, 1)

            with pe.Fori(0, B) as b:
                for s in range(SLOTS):
                    for u in tiles1(s):
                        use(b, u)
                for u in stage2():
                    use(b, u)
                for n in range(NSTEP):
                    scores(b, n, 0)
                    scores(b, n, 1)
                    if n:
                        attend(b, n - 1)
                    scores(b, n, 2)
                    scores(b, n, 3)
                    for u in filler(n // STEPS, n % STEPS):
                        use(b, u)
                attend(b, NSTEP - 1)
                for s in range(SLOTS):
                    for u in tiles4(s):
                        use(b, u)


_INS = ["L0_attn_x", "L0_attn_Wqkv", "L0_attn_bqkv", "L0_attn_Wo", "L0_attn_bo", "L0_ffn_weight", "L0_ffn_bias"]
_OUTS = [((4, 1024, 512), "float32")]


def kernel(**inputs):
    import numpy as _np
    import concourse.bacc as _bacc
    from concourse import mybir as _mybir
    from concourse.bass_utils import run_bass_kernel_spmd as _run

    nc = _bacc.Bacc("TRN2", target_bir_lowering=False, num_devices=1)
    arrays, args = {}, []
    for name in _INS:
        a = _np.ascontiguousarray(inputs[name])
        arrays[f"in_{name}_dram"] = a
        args.append(nc.dram_tensor(f"in_{name}_dram", a.shape, _mybir.dt.from_np(a.dtype), kind="ExternalInput").ap())
    for i, (shape, dtype) in enumerate(_OUTS):
        dt = _mybir.dt.from_np(_np.dtype(dtype))
        args.append(nc.dram_tensor(f"out_{i}_dram", shape, dt, kind="ExternalOutput").ap())
    macaron_kernel(nc, *args)
    r = _run(nc, [arrays], core_ids=[0])
    got = tuple(r.results[0][f"out_{i}_dram"] for i in range(len(_OUTS)))
    return got[0]
```

```python
from contextlib import ExitStack

import concourse.bass as bass
from concourse import mybir

F32 = mybir.dt.float32
F32R = mybir.dt.float32r
BF16 = mybir.dt.bfloat16
ALU = mybir.AluOpType
ACT = mybir.ActivationFunctionType
AX = mybir.AxisListType.X

P = 128
B, S, D = 4, 1024, 512
HEADS, HD = 16, 32
TILES = S // P
KC = D // P
GROUPS = HEADS // 4
CW = 512
CHUNKS = S // CW
QPC = CW // P
SCALE = float(HD) ** -0.5
EPS_LN = 1e-5
EPS_FFN = 1e-10
NEG = -1e30
KQ = 3 * HD
HI, LO = 0, 1
K_, Q_ = 0, 1
W_COLUMN = {K_: D, Q_: 0}

RING = 4
STEPS = QPC + 2 * QPC


def step_of(i):
    c, kb = (0, i) if i < QPC else (1, i - QPC)
    return c, kb, max(0, P * kb - CW * c)


def diagonal(i):
    c, kb, _ = step_of(i)
    return kb >= QPC * c


def maxima(g, c):
    return [("A", g, h, QPC * c + r, kc) for h in range(4) for r in range(QPC) for kc in range(c + 1)]


def pieces(g):
    return [("P", g, K_, 0), ("P", g, Q_, 0), ("P", g, K_, 1), ("P", g, Q_, 1)]


AHEAD = 24
AHEAD_0 = 24


def share(work, n, i):
    part = work[len(work) * i // n:len(work) * (i + 1) // n]
    return part[:(len(part) + 1) // 2], part[(len(part) + 1) // 2:]


def filler(g, i):
    first, second = [], []
    if i < 2:
        first, second = share(maxima(g, 1)[AHEAD if g else AHEAD_0:], 2, i)
    elif i == 2:
        first = [("M", g, 1)]
    if g + 1 == GROUPS:
        if i >= STEPS - FIRST_SLOT:
            return SLOTS[i - STEPS + FIRST_SLOT], []
        return first, second
    if i < 4:
        return first + second, [pieces(g + 1)[i]]
    first, second = share(maxima(g + 1, 0) + maxima(g + 1, 1)[:AHEAD], STEPS - 4, i - 4)
    return first, second + ([("M", g + 1, 0)] if i == 8 else [])


def norm_parts(g, i):
    if i <= QPC:
        return 2 * g - 1, [i - 1] if g and i else []
    per = 2 if g + 1 == GROUPS else 1
    return 2 * g, [n for n in range(per * (i - QPC - 1), per * (i - QPC)) if n < 4]


def between():
    a, a1 = maxima(0, 0), maxima(0, 1)
    p = pieces(0)
    return [
        [("O", 0)],
        [("O", 1)],
        [("O", 2), ("T3", 0)],
        [("F2", 0), ("O", 3), ("T3", 1)],
        [("F2", 1), ("T3", 2)],
        [("F2", 2), ("T3", 3)],
        [("F2", 3), ("O", 4), ("T1", 0)],
        [("O", 5), ("F1", 0), ("T1", 1)],
        [("O", 6), ("F1", 1), ("T3", 4), ("T1", 2)],
        [("F2", 4), ("O", 7), ("F1", 2), ("T3", 5), ("T1", 3), ("T2", 0)],
        [("F2", 5), ("F1", 3), ("T3", 6), ("T2", 1)],
        [("F2", 6), ("T3", 7), ("T2", 2), ("V", 0)],
        [("F2", 7), ("T1", 4), ("T2", 3), ("V", 1)],
        [("F1", 4), ("T1", 5), p[0]],
        [("F1", 5), ("T1", 6), ("V", 2), p[1]],
        [("F1", 6), ("T1", 7), ("T2", 4), ("V", 3)],
        [("F1", 7), ("T2", 5), ("V", 4)],
        [("T2", 6), a[0], a[1], ("V", 5), a[2], a[3]],
        [("T2", 7), a[4], a[5], a[6], a[7]],
        [a[8], p[2], a[9], a[10], a[11]],
        [a[12], p[3], a[13], a[14], a[15]],
        [("M", 0, 0), ("V", 6)],
        [("V", 7)] + a1[:8],
        a1[8:AHEAD_0],
    ]


SLOTS = between()
FIRST_SLOT = 4
ENDING = ("O", "T3", "F2")


class Order:

    def __init__(self, uses, slots, before, split_before):
        self.slots, self.before, self.split_before = slots, before, split_before
        self.uses = uses
        self.at = {u: n for n, u in enumerate(uses)}
        self.split = {u: n for n, u in enumerate([u for u in uses if u[0] in ("T1", "T2", "T3", "P", "M")])}
        assert len(self.at) == len(uses)


def flat(slots):
    return [u for s in slots for u in s]


SETUP_USES = 6
GROUP_USES = [u for g in range(GROUPS) for i in range(STEPS) for part in filler(g, i) for u in part]
HEAD = Order(flat([[u for u in s if u[0] not in ENDING] for s in SLOTS[FIRST_SLOT:]]),
             [[u for u in s if u[0] not in ENDING] for s in SLOTS], SETUP_USES, 0)
_BASE, _SPLIT = SETUP_USES + len(HEAD.uses), len(HEAD.split)
BODY = Order(GROUP_USES + flat(SLOTS[FIRST_SLOT:]), SLOTS, _BASE, _SPLIT)
TAIL = Order(GROUP_USES + flat([[u for u in s if u[0] in ENDING] for s in SLOTS[FIRST_SLOT:]]),
             [[u for u in s if u[0] in ENDING] for s in SLOTS], _BASE, _SPLIT)
R, NSPLIT = len(BODY.uses), len(BODY.split)
assert R % RING == 0

NEXT_W = [("WV", k) for k in range(KC)] + [("QK", g, j) for g in (0, 1) for j in (K_, Q_)]
WCHUNKS = [("QK", g, j) for g in (2, 3) for j in (K_, Q_)] + [("WO", g) for g in range(KC)] + NEXT_W
W, FIRST_W = len(WCHUNKS), len(NEXT_W)
WAT = {w: FIRST_W + n for n, w in enumerate(WCHUNKS)}
SPLIT_SLOTS = {4: NEXT_W[0], 5: NEXT_W[1], 6: NEXT_W[2], 7: NEXT_W[3], 8: NEXT_W[4], 9: NEXT_W[5],
               20: NEXT_W[6], 21: NEXT_W[7]}
SPLIT_STEPS = {(0, 4): WCHUNKS[0], (0, 5): WCHUNKS[1], (1, 4): WCHUNKS[2], (1, 5): WCHUNKS[3],
               (3, 4): WCHUNKS[4], (3, 5): WCHUNKS[5], (3, 6): WCHUNKS[6], (3, 7): WCHUNKS[7]}
LOAD_STEPS = {(0, 1): WCHUNKS[0], (0, 2): WCHUNKS[1], (1, 1): WCHUNKS[2], (1, 2): WCHUNKS[3],
              (2, 1): WCHUNKS[4], (2, 2): WCHUNKS[5], (3, 5): WCHUNKS[6], (3, 6): WCHUNKS[7]}
NS = 4 * STEPS * GROUPS
NSTEP = STEPS * GROUPS
NDIAG = 2 * QPC * GROUPS
NCH = CHUNKS * GROUPS


def macaron_kernel(nc, x, wqkv, bqkv, wo, bo, wf, bf, out):
    with ExitStack() as ctx:
        def sb(name, shape, dt=F32):
            return ctx.enter_context(nc.sbuf_tensor(name, shape, dt))

        def sem(name):
            return ctx.enter_context(nc.semaphore(name))

        xt = sb("xt", [P, TILES, D])
        wfT = sb("wfT", [P, KC, D], F32R)
        wqk = sb("wqk", [P, 2, 2, KC, P], F32R)
        stage = sb("stage", [P, 2, D])
        hT = sb("hT", [P, 2, KC, S], F32R)
        hts = sb("hts", [P, 2, 2, KC, P], F32R)
        hn = sb("hn", [P, 3, D])
        v = sb("v", [P, TILES, D])
        nat = sb("nat", [P, 2, 2, CW], F32R)
        kst = [sb(f"kst{n}", [P, CHUNKS, 4, CW], F32R) for n in range(2)]
        qst = [sb(f"qst{n}", [P, CHUNKS, 4, CW], F32R) for n in range(2)]
        prob = sb("prob", [P, 2, 4, CW])
        o32 = sb("o32", [P, 4, CW])
        rec = sb("rec", [P, CW])
        junk = sb("junk", [P, 2, CW], BF16)
        mask = sb("mask", [P, CW], BF16)
        ident = sb("ident", [P, P])
        ones = sb("ones", [P, P])
        hb = sb("hb", [P, D])
        bo2 = sb("bo2", [P, D])
        bqk = sb("bqk", [P, 3 * KC])
        small = sb("small", [P, 8])
        st6 = sb("st6", [P, 3, 2, 6])
        mv = sb("mv", [P, 3, TILES, 2])
        ve = sb("ve", [P, 3, TILES])
        rstd = sb("rstd", [P, 3, TILES])
        nmr = sb("nmr", [P, 3, TILES])
        mst = sb("mst", [P, 3, 4 * QPC])
        mcol = sb("mcol", [P, 4 * QPC])
        mrow = sb("mrow", [4 * QPC, 2, 2, P], F32R)
        scr = nc.dram_tensor("stack_scratch", [2, CHUNKS, 2, HD, 4, CW], F32, kind="Internal").ap()

        wvT, woT = qst[1], qst[0]
        bank = [ctx.enter_context(nc.psum_tensor(f"bank{n}", [P, CW], F32)) for n in range(8)]
        sbank, accv, accs = bank[4:6], bank[6], bank[7]

        ring_full, ring_free = sem("ring_full"), sem("ring_free")
        hi_done = sem("hi_done")
        s_full, s_exp = sem("s_full"), sem("s_exp")
        masked, step_used = sem("masked"), sem("step_used")
        acc_free = sem("acc_free")
        rec_done, norm_done = sem("rec_done"), sem("norm_done")
        o_hi, o_split = sem("o_hi"), sem("o_split")
        w_hi, w_split = sem("w_hi"), sem("w_split")
        st_done = [sem(f"st_done{n}") for n in range(3)]
        mv_done = [sem(f"mv_done{n}") for n in range(3)]
        ve_done = [sem(f"ve_done{n}") for n in range(3)]
        rs_done = [sem(f"rs_done{n}") for n in range(3)]
        nm_done = [sem(f"nm_done{n}") for n in range(3)]
        hn_done = [sem(f"hn_done{n}") for n in range(3)]
        xb_done = [sem(f"xb_done{n}") for n in range(3)]
        mcol_done = sem("mcol_done")
        x_in = [sem(f"x_in{t}") for t in range(TILES)]
        x_out = [sem(f"x_out{t}") for t in range(TILES)]
        staged = [sem(f"staged{n}") for n in range(2)]
        scr_in = sem("scr_in")
        stk_in = [[sem(f"stk_in{j}{c}") for c in range(CHUNKS)] for j in range(2)]
        mrow_in = [sem(f"mrow_in{c}") for c in range(CHUNKS)]
        set_wf, set_wo, set_b = sem("set_wf"), sem("set_wo"), sem("set_b")
        set_pool, set_dve = sem("set_pool"), sem("set_dve")

        def used(o, b, u):
            return (0 if o is HEAD else b * R) + (o.before + o.at[u] + 1)

        def started(b):
            return b * R + BODY.before

        def split(o, b, u):
            return (0 if o is HEAD else b * NSPLIT) + (o.split_before + o.split[u] + 1)

        def ring(o, u):
            return bank[(o.before + o.at[u]) % RING][:, :]

        def tile(b, t):
            return b * TILES + (t + 1)

        def exps(b, n):
            return b * NS + (n + 3)

        def stepped(b, n):
            return b * NSTEP + (n + 3)

        def evacuated(b, n):
            return b * NCH + (n + 2)

        def normed(b, n):
            return b * NCH + (n + 2)

        def out_split(b, n):
            return b * NCH + (n + 5)

        def wsplit(o, b, w):
            return NEXT_W.index(w) + 1 if o is HEAD else b * W + (WAT[w] + 1)

        def group(b, g, per):
            return b * (GROUPS * per) + per * (g + 1)

        def source(w):
            if w[0] == "QK":
                at = W_COLUMN[w[2]] + P * w[1]
                return wqkv[:, at:at + P].rearrange("(k p) n -> p k n", p=P)
            if w[0] == "WO":
                return wo[P * w[1]:P * w[1] + P, :]
            return wqkv[P * w[1]:P * w[1] + P, 2 * D:3 * D]

        def target(w, part):
            if w[0] == "QK":
                return wqk[:, part, w[2], :, :].rearrange("p k n -> p (k n)")
            return (woT if w[0] == "WO" else wvT)[:, part, w[1], :]

        def stage_as(w, n):
            return stage[:, n, :].rearrange("p (k n) -> p k n", k=KC) if w[0] == "QK" else stage[:, n, :]

        def blocks(o, u):
            return ring(o, u).rearrange("p (k n) -> p k n", k=KC)

        def bias_of(j, g):
            return bqk[:, KC * (j == K_) + g:KC * (j == K_) + g + 1]

        dve_past, pool_past, sp_past = sem("dve_past"), sem("pool_past"), sem("sp_past")
        block = ctx.enter_context(nc.Block())

        @block.sync
        def _(sp):
            sp.dma_start(prob[:, 0, :, :], wf.rearrange("(k p) n -> p k n", p=P)).then_inc(set_wf, 16)
            sp.dma_start(xt[:, 0, :], x[0, 0:P, :]).then_inc(x_in[0], 16)
            sp.dma_start(hb[:, :], bf.partition_broadcast(P)).then_inc(set_b, 16)
            sp.dma_start(bo2[:, :], bo.partition_broadcast(P)).then_inc(set_b, 16)
            sp.dma_start(bqk[:, :], bqkv.rearrange("(k p) -> p k", p=P), allow_slow_non_contiguous=True).then_inc(set_b, 16)
            sp.dma_start(v[:, 0:KC, :], wo.rearrange("(k p) n -> p k n", p=P)).then_inc(set_wo, 16)
            for t in range(1, TILES):
                sp.dma_start(xt[:, t, :], x[0, P * t:P * t + P, :]).then_inc(x_in[t], 16)
            def load_weights(o, b, w):
                n = wsplit(o, b, w) - 1
                slot = (NEXT_W.index(w) if o is HEAD else WAT[w]) % 2
                if o is not HEAD or NEXT_W.index(w) >= 2:
                    sp.wait_ge(w_split, n - 1)
                sp.dma_start(stage_as(w, slot), source(w)).then_inc(staged[slot], 16)

            def stack(o, b, u, first_free):
                _, g, j, c = u
                nb = b if o.at[u] < len(GROUP_USES) and o is not HEAD else b + 1
                lay = scr[j, c]
                if first_free is not None:
                    sp.wait_ge(s_full, first_free)
                    sp.sem_inc(sp_past, 1)
                sp.wait_ge(hi_done, split(o, b, u))
                sp.dma_start(lay[HI].rearrange("r h n -> h r n"), nat[:, j, HI, :].bitcast(F32)).then_inc(scr_in, 16)
                sp.wait_ge(ring_free, used(o, b, u))
                sp.dma_start(lay[LO].rearrange("r h n -> h r n"), nat[:, j, LO, :].bitcast(F32)).then_inc(scr_in, 16)
                n = pieces(g).index(u)
                sp.wait_ge(scr_in, nb * (GROUPS * 128) + (128 * g + 32 * (n + 1)))
                both = lay.rearrange("l r h n -> (l r) h n")
                dst = (kst, qst)[j][g % 2]
                pair, single = ((0, 2 * HD), (2 * HD, KQ)) if j == K_ else ((HD, KQ), (0, HD))
                sp.dma_start(dst[pair[0]:pair[1], c, :, :].bitcast(F32), both).then_inc(stk_in[j][c], 16)
                sp.dma_start(dst[single[0]:single[1], c, :, :].bitcast(F32), both[0:HD]).then_inc(stk_in[j][c], 16)

            def rows(o, b, u):
                _, g, c = u
                sp.wait_ge(ring_free, used(o, b, u))
                for part in (HI, LO):
                    row = KQ + part
                    sp.dma_start(qst[g % 2][row:row + 1, c, :, :].rearrange("p h n -> p (h n)").bitcast(F32),
                                 mrow[:, c, part, :].bitcast(F32)).then_inc(mrow_in[c], 16)

            def event(o, b, u):
                if u[0] == "P":
                    stack(o, b, u, b * NS + 4 * STEPS * (u[1] - 1) if u[1] >= 2 else None)
                elif u[0] == "M":
                    rows(o, b, u)
                elif u[0] == "F2":
                    t = u[1]
                    sp.wait_ge(ring_free, used(o, b, u))
                    sp.sem_inc(sp_past, 1)
                    sp.dma_start(out[b, P * t:P * t + P, :], xt[:, t, :]).then_inc(x_out[t], 16)

            def slot(o, b, q):
                if o is BODY and q:
                    for u in o.slots[q - 1]:
                        if u[0] == "F2":
                            t = u[1]
                            sp.wait_ge(x_out[t], b * 16 + 16)
                            sp.sem_inc(sp_past, 1)
                            sp.dma_start(xt[:, t, :], x[b + 1, P * t:P * t + P, :]).then_inc(x_in[t], 16)
                for u in o.slots[q]:
                    event(o, b, u)
                if o is not TAIL and q in SPLIT_SLOTS:
                    load_weights(o, b, SPLIT_SLOTS[q])

            def sequence(o, b):
                for g in range(GROUPS):
                    for i in range(STEPS):
                        if g == GROUPS - 1 and i >= STEPS - FIRST_SLOT:
                            slot(o, b, i - STEPS + FIRST_SLOT)
                        else:
                            for part in filler(g, i):
                                for u in part:
                                    event(o, b, u)
                        if (g, i) in LOAD_STEPS:
                            load_weights(o, b, LOAD_STEPS[g, i])
                for q in range(FIRST_SLOT, len(SLOTS)):
                    slot(o, b, q)

            for q in range(FIRST_SLOT, len(SLOTS)):
                slot(HEAD, -1, q)
            with sp.Fori(0, B - 1) as b:
                sequence(BODY, b)
            sequence(TAIL, B - 1)
            for t in range(TILES):
                sp.wait_ge(x_out[t], 16 * B)

        @block.gpsimd
        def _(pool):
            nc.gpsimd.memset(ident[:, :], 0.0).then_inc(set_pool, 1)
            nc.gpsimd.memset(mask[:, :], 0.0).then_inc(set_pool, 1)
            nc.gpsimd.memset(ones[:, :], 1.0).then_inc(set_pool, 1)
            nc.gpsimd.memset(small[:, 4:5], -0.5).then_inc(set_pool, 1)
            pool.wait_ge(set_pool, 4)
            nc.gpsimd.affine_select(out=ident[:, :], in_=ident[:, :], compare_op=ALU.not_equal, fill=1.0, base=0,
                                    pattern=[[-1, P]], channel_multiplier=1).then_inc(set_pool, 1)
            nc.gpsimd.affine_select(out=mask[:, CW - P:CW], in_=mask[:, CW - P:CW], compare_op=ALU.is_ge, fill=NEG,
                                    base=0, pattern=[[-1, P]], channel_multiplier=1).then_inc(set_pool, 1)
            pool.wait_ge(set_pool, 6)
            pool.wait_ge(set_b, 48)
            nc.gpsimd.tensor_scalar(hb[:, :], hb[:, :], 0.5, 0.0, ALU.mult, ALU.add).then_inc(o_split, 4)
            pool.wait_ge(o_split, 4)

            def weights(o, b, w):
                n = NEXT_W.index(w) if o is HEAD else WAT[w]
                slot = n % 2
                pool.wait_ge(staged[slot], (0 if o is HEAD else b * (W * 8)) + 16 * (n // 2 + 1))
                pool.sem_inc(pool_past, 1)
                nc.gpsimd.tensor_copy(target(w, HI), stage[:, slot, :]).then_inc(w_hi, 1)
                pool.wait_ge(w_hi, wsplit(o, b, w))
                nc.gpsimd.tensor_tensor(target(w, LO), stage[:, slot, :], target(w, HI).bitcast(F32), ALU.subtract)\
                    .then_inc(w_split, 1)

            def rsqrt(b, l, t):
                pool.wait_ge(mv_done[l], tile(b, t))
                pool.sem_inc(pool_past, 1)
                nc.gpsimd.tensor_scalar(ve[:, l, t:t + 1], mv[:, l, t, 1:2], 1.0, EPS_LN, ALU.mult, ALU.add)\
                    .then_inc(ve_done[l], 1)
                pool.wait_ge(ve_done[l], tile(b, t))
                nc.gpsimd.tensor_tensor(rstd[:, l, t:t + 1], ve[:, l, t:t + 1], small[:, 4:5], ALU.pow)\
                    .then_inc(rs_done[l], 1)

            def add_bias(b, l, t):
                pool.wait_ge(hn_done[l], tile(b, t))
                nc.gpsimd.tensor_tensor(xt[:, t, :], xt[:, t, :], (bo2 if l == 1 else hb)[:, :], ALU.add)\
                    .then_inc(xb_done[l], 1)

            def split_output(b, n):
                g, c = n // CHUNKS, n % CHUNKS
                pool.wait_ge(norm_done, normed(b, n))
                hi, lo = (hT[:, part, g, CW * c:CW * c + CW] for part in (HI, LO))
                pool.sem_inc(pool_past, 1)
                nc.gpsimd.tensor_copy(hi, o32[:, n % 4, :]).then_inc(o_hi, 1)
                pool.wait_ge(o_hi, b * NCH + (n + 1))
                nc.gpsimd.tensor_tensor(lo, o32[:, n % 4, :], hi.bitcast(F32), ALU.subtract).then_inc(o_split, 1)

            def step(b, g, i):
                if diagonal(i):
                    n = STEPS * g + i
                    off = step_of(i)[2]
                    pool.wait_ge(s_exp, exps(b, 4 * n + 3))
                    part = prob[:, n % 2, :, off:off + P]
                    pool.sem_inc(pool_past, 1)
                    nc.gpsimd.affine_select(out=part, in_=part, compare_op=ALU.is_ge, fill=0.0, base=0,
                                            pattern=[[0, 4], [1, P]], channel_multiplier=-1).then_inc(masked, 1)

            def slot(o, b, q):
                now, before = o.slots[q], o.slots[q - 1] if q else []
                after = o.slots[q + 1] if q + 1 < len(o.slots) else []
                for kind, t in [u for u in now if u[0] in ("F1", "O")]:
                    rsqrt(*((b + 1, 1) if kind == "F1" else (b, 2)), t)
                for t in [u[1] for u in after if u[0] == "T1"]:
                    rsqrt(b + 1, 0, t)
                for t in [u[1] for u in now if u[0] == "T1"]:
                    add_bias(b + 1, 0, t)
                for kind, t in [u for u in before if u[0] in ("F1", "O")]:
                    add_bias(*((b + 1, 1) if kind == "F1" else (b, 2)), t)
                if o is not TAIL and q in SPLIT_SLOTS:
                    if q == FIRST_SLOT and o is BODY:
                        pool.wait_ge(s_full, b * NS + NS)
                    if q == 20:
                        pool.wait_ge(ring_full, used(o, b, pieces(0)[-1]))
                    weights(o, b, SPLIT_SLOTS[q])
                if q == 4 and o is not HEAD:
                    split_output(b, 7)

            def sequence(o, b):
                for g in range(GROUPS):
                    for i in range(STEPS):
                        step(b, g, i)
                        if i == 3 and g == 2:
                            pool.wait_ge(ring_full, used(o, b, pieces(3)[-1]))
                            for n in range(4):
                                split_output(b, n)
                        if i == 9 and g == 2:
                            split_output(b, 4)
                        if i == 5 and g == 3:
                            split_output(b, 5)
                        if i == 7 and g == 3:
                            split_output(b, 6)
                        if (g, i) in SPLIT_STEPS:
                            if i == 4 and g < 2:
                                pool.wait_ge(ring_full, used(o, b, pieces(g + 1)[-1]))
                            if i == 4 and g == 3:
                                pool.wait_ge(s_full, b * NS + 3 * 4 * STEPS)
                            weights(o, b, SPLIT_STEPS[g, i])
                        if g == GROUPS - 1 and i >= STEPS - FIRST_SLOT:
                            slot(o, b, i - STEPS + FIRST_SLOT)
                for q in range(FIRST_SLOT, len(SLOTS)):
                    slot(o, b, q)

            for q in range(FIRST_SLOT, len(SLOTS)):
                slot(HEAD, -1, q)
            with pool.Fori(0, B - 1) as b:
                sequence(BODY, b)
            sequence(TAIL, B - 1)

        @block.vector
        def _(dve):
            def filled(n):
                return dve.wait_ge(ring_full, n)

            wn, wt = prob[:, 0, :, :], prob[:, 1, :, :]
            dve.wait_ge(set_wf, 16)
            nc.vector.tensor_reduce(small[:, 0:1], wn.rearrange("p k n -> p (k n)"), AX, ALU.add,
                                    apply_absolute_value=True).then_inc(set_dve, 1)
            filled(1)
            nc.vector.tensor_scalar(small[:, 1:2], bank[0][:, 0:1], 1.0 / (D * D), None, ALU.mult).then_inc(ring_free, 1)
            dve.wait_ge(ring_free, 1)
            nc.vector.tensor_scalar(small[:, 2:3], small[:, 1:2], EPS_FFN, 0.5, ALU.add, ALU.mult).then_inc(set_dve, 1)
            nc.vector.tensor_scalar(small[:, 5:6], small[:, 1:2], 0.5, None, ALU.mult).then_inc(set_dve, 1)
            dve.wait_ge(set_dve, 3)
            nc.vector.tensor_scalar(small[:, 3:4], small[:, 2:3], -1.0, None, ALU.mult).then_inc(set_dve, 1)
            dve.wait_ge(set_dve, 4)
            flat = [a.rearrange("p k n -> p (k n)") for a in (wn, wt)]
            nc.vector.tensor_scalar(flat[1], flat[0], small[:, 3:4], None, ALU.is_lt).then_inc(set_dve, 1)
            dve.wait_ge(set_dve, 5)
            nc.vector.scalar_tensor_tensor(flat[1], flat[0], small[:, 2:3], flat[1], ALU.is_gt, ALU.subtract)\
                .then_inc(set_dve, 1)
            dve.wait_ge(set_b, 48)
            dve.wait_ge(set_pool, 6)
            for k in range(KC):
                nc.vector.tensor_scalar(o32[:, 0, P * k:P * k + P], ones[:, :], bqk[:, 2 * KC + k:2 * KC + k + 1], None,
                                        ALU.mult).then_inc(set_dve, 1)
            for n in range(2):
                nc.vector.memset(kst[n][KQ:KQ + 2, :, :, :].bitcast(F32), 1.0).then_inc(set_dve, 1)
            nc.vector.memset(rec[:, :], 0.0).then_inc(norm_done, 1)
            dve.wait_ge(norm_done, 1)
            for k in range(KC):
                filled(2 + k)
                nc.vector.tensor_copy(wfT[:, k, :], bank[(1 + k) % RING][:, :]).then_inc(ring_free, 1)
            filled(6)
            nc.vector.tensor_tensor(bo2[:, :], bank[5 % RING][:, :], bo2[:, :], ALU.add).then_inc(ring_free, 1)

            def stats(o, run, b, l, t):
                if l == 0:
                    dve.wait_ge(x_in[t], b * 16 + 16)
                else:
                    dve.wait_ge(ring_free, used(o, run, (("F1", "O")[l - 1], t)))
                s = st6[:, l, t % 2, :]
                nc.vector.bn_stats(s, xt[:, t, :]).then_inc(st_done[l], 1)
                dve.wait_ge(st_done[l], tile(b, t))
                dve.sem_inc(dve_past, 1)
                nc.vector.bn_aggr(mv[:, l, t, :], s).then_inc(mv_done[l], 1)

            def shift(b, l, t):
                dve.wait_ge(rs_done[l], tile(b, t))
                nc.vector.scalar_tensor_tensor(nmr[:, l, t:t + 1], mv[:, l, t, 0:1], -1.0, rstd[:, l, t:t + 1],
                                               ALU.mult, ALU.mult).then_inc(nm_done[l], 1)

            def low(o, b, u, dst, src, hi, first=None):
                dve.wait_ge(hi_done, split(o, b, u))
                if first is None:
                    i = nc.vector.tensor_tensor(dst, src, hi.bitcast(F32), ALU.subtract)
                else:
                    i = nc.vector.scalar_tensor_tensor(dst, src, first[0], hi.bitcast(F32), first[1], ALU.subtract)
                i.then_inc(ring_free, 1)

            def residual(o, b, u, nb, l):
                t = u[1]
                dve.wait_ge(ring_full, used(o, b, u))
                dve.wait_ge(xb_done[l], tile(nb, t))
                if l == 1:
                    nc.vector.tensor_tensor(xt[:, t, :], ring(o, u), xt[:, t, :], ALU.add).then_inc(ring_free, 1)
                else:
                    nc.vector.scalar_tensor_tensor(xt[:, t, :], ring(o, u), small[:, 5:6], xt[:, t, :],
                                                   ALU.mult, ALU.add).then_inc(ring_free, 1)

            def maximum(o, b, u):
                _, g, h, qb, kc = u
                c, r = qb // QPC, qb % QPC
                dve.wait_ge(ring_full, used(o, b, u))
                at = 4 * h + r
                if kc < c:
                    nc.vector.tensor_reduce(mst[:, 1, at:at + 1], ring(o, u), AX, ALU.max).then_inc(ring_free, 1)
                else:
                    n = P * (r + 1)
                    dve.wait_ge(ring_free, used(o, b, u) - 2)
                    dve.sem_inc(dve_past, 1)
                    nc.vector.tensor_tensor_reduce(junk[:, o.at[u] % 2, 0:n], ring(o, u)[:, 0:n], mask[:, CW - n:CW],
                                                   1.0, -3e38, ALU.add, ALU.max, mst[:, 2 * c, at:at + 1])\
                        .then_inc(ring_free, 1)
                if u == maxima(g, 1)[-1]:
                    dve.wait_ge(ring_free, used(o, b, u))
                    nc.vector.tensor_tensor(mcol[:, :], mst[:, 1, :], mst[:, 2, :], ALU.max).then_inc(mcol_done, 1)

            def invert(b, n, part):
                if part == 0:
                    dve.wait_ge(acc_free, evacuated(b, n))
                at = slice(P * part, P * part + P)
                nc.vector.reciprocal(rec[:, at], rec[:, at]).then_inc(rec_done, 1)

            def normalise(b, n):
                dve.wait_ge(rec_done, b * (4 * NCH) + 4 * (n + 1))
                nc.vector.tensor_tensor(o32[:, n % 4, :], o32[:, n % 4, :], rec[:, :], ALU.mult).then_inc(norm_done, 1)

            def use(o, b, u):
                if u[0] == "A":
                    maximum(o, b, u)
                elif u[0] == "V":
                    dve.wait_ge(ring_full, used(o, b, u))
                    nc.vector.tensor_copy(v[:, u[1], :], ring(o, u)).then_inc(ring_free, 1)
                elif u[0] == "P":
                    _, g, j, c = u
                    low(o, b, u, nat[:, j, LO, :], ring(o, u), nat[:, j, HI, :], (bias_of(j, g), ALU.add))
                elif u[0] == "M":
                    c = u[2]
                    low(o, b, u, mrow[:, c, LO, :], ring(o, u)[0:4 * QPC, 0:P], mrow[:, c, HI, :], (-1.0, ALU.mult))
                elif u[0] == "T2":
                    at = slice(P * u[1], P * u[1] + P)
                    low(o, b, u, hT[:, LO, :, at], blocks(o, u), hT[:, HI, :, at])
                elif u[0] in ("T1", "T3"):
                    which = (u[0] == "T3") * 1
                    low(o, b, u, hts[:, which, LO, :, :], blocks(o, u), hts[:, which, HI, :, :])
                else:
                    residual(o, b, u, *{"F1": (b + 1, 0), "O": (b, 1), "F2": (b, 2)}[u[0]])

            def slot(o, b, q, chunk=None):
                parts = 4 if chunk is not None else 0
                for u in o.slots[q]:
                    use(o, b, u)
                    if u[0] == "F1":
                        stats(o, b, b + 1, 1, u[1])
                    if u[0] == "O":
                        stats(o, b, b, 2, u[1])
                for part in range(parts):
                    invert(b, chunk, part)
                if parts:
                    normalise(b, chunk)
                after = [u[1] for u in o.slots[q + 1] if u[0] == "T1"] if q + 1 < len(o.slots) else []
                for t in after:
                    stats(o, b, b + 1, 0, t)
                for kind, t in [u for u in o.slots[q] if u[0] in ("F1", "O")]:
                    shift(*((b + 1, 1) if kind == "F1" else (b, 2)), t)
                for t in after:
                    shift(b + 1, 0, t)

            def sequence(o, b):
                for n in range(NSTEP):
                    g, i = n // STEPS, n % STEPS
                    if g == GROUPS - 1 and i >= STEPS - FIRST_SLOT:
                        slot(o, b, i - STEPS + FIRST_SLOT)
                        continue
                    first, second = filler(g, i)
                    for u in first:
                        use(o, b, u)
                    chunk, parts = norm_parts(g, i)
                    for part in parts:
                        invert(b, chunk, part)
                    for u in second:
                        use(o, b, u)
                    if 3 in parts:
                        normalise(b, chunk)
                for q in range(FIRST_SLOT, len(SLOTS)):
                    slot(o, b, q, NCH - 1 if q == FIRST_SLOT else None)

            for q in range(FIRST_SLOT, len(SLOTS)):
                slot(HEAD, -1, q)
            with dve.Fori(0, B - 1) as b:
                sequence(BODY, b)
            sequence(TAIL, B - 1)

        @block.scalar
        def _(act):
            act.wait_ge(set_pool, 6)
            nc.scalar.activation(small[:, 6:7], ones[:, 0:1], ACT.Exp).then_inc(s_exp, 2)
            nc.scalar.activation(small[:, 7:8], ones[:, 0:1], ACT.Identity).then_inc(acc_free, 1)
            act.wait_ge(set_b, 48)

            def normal(b, l, t):
                act.wait_ge(nm_done[l], tile(b, t))
                nc.scalar.activation(hn[:, l, :], xt[:, t, :], ACT.Identity, bias=nmr[:, l, t:t + 1],
                                     scale=rstd[:, l, t:t + 1]).then_inc(hn_done[l], 1)

            def high(o, b, u):
                kind = u[0]
                act.wait_ge(ring_full, used(o, b, u))
                if kind == "P":
                    _, g, j, c = u
                    n = pieces(g).index(u)
                    if g or n >= 2:
                        nb = b if g else b + 1
                        act.wait_ge(scr_in, nb * (GROUPS * 128) + (128 * g + 32 * (n - 1)))
                    i = nc.scalar.activation(nat[:, j, HI, :], ring(o, u), ACT.Identity, bias=bias_of(j, g))
                elif kind == "M":
                    i = nc.scalar.activation(mrow[:, u[2], HI, :], ring(o, u)[0:4 * QPC, 0:P], ACT.Identity, scale=-1.0)
                elif kind == "T2":
                    i = nc.scalar.activation(hT[:, HI, :, P * u[1]:P * u[1] + P], blocks(o, u), ACT.Identity)
                else:
                    i = nc.scalar.activation(hts[:, (kind == "T3") * 1, HI, :, :], blocks(o, u), ACT.Identity)
                i.then_inc(hi_done, 1)

            def evacuate(b, n):
                act.wait_ge(step_used, stepped(b, n // 2 * STEPS + (QPC - 1, STEPS - 1)[n % 2]))
                act.wait_ge(norm_done, normed(b, n - 1))
                nc.scalar.activation(rec[:, :], accs[:, :], ACT.Identity)
                act.wait_ge(o_split, out_split(b, n - 4))
                nc.scalar.activation(o32[:, n % 4, :], accv[:, :], ACT.Identity).then_inc(acc_free, 1)

            def slot(o, b, q):
                for u in o.slots[q]:
                    if u in o.split:
                        high(o, b, u)
                for kind, t in [u for u in (o.slots[q - 1] if q else []) if u[0] in ("F1", "O")]:
                    normal(*((b + 1, 1) if kind == "F1" else (b, 2)), t)
                for t in [u[1] for u in (o.slots[q + 1] if q + 1 < len(o.slots) else []) if u[0] == "T1"]:
                    normal(b + 1, 0, t)

            def sequence(o, b):
                for n in range(NSTEP):
                    g, i = n // STEPS, n % STEPS
                    off = step_of(i)[2]
                    act.wait_ge(step_used, stepped(b, n - 2))
                    for h in range(4):
                        act.wait_ge(s_full, b * NS + (4 * n + h + 1))
                        nc.scalar.activation(prob[:, n % 2, h, off:CW], sbank[h % 2][:, off:CW], ACT.Exp, scale=SCALE)\
                            .then_inc(s_exp, 1)
                    if g == GROUPS - 1 and i >= STEPS - FIRST_SLOT:
                        slot(o, b, i - STEPS + FIRST_SLOT)
                    else:
                        for part in filler(g, i):
                            for u in part:
                                if u in o.split:
                                    high(o, b, u)
                    if i == 0 and g:
                        evacuate(b, 2 * g - 1)
                    if i == QPC:
                        evacuate(b, 2 * g)
                evacuate(b, NCH - 1)
                for q in range(FIRST_SLOT, len(SLOTS)):
                    slot(o, b, q)

            for q in range(FIRST_SLOT, len(SLOTS)):
                slot(HEAD, -1, q)
            with act.Fori(0, B - 1) as b:
                sequence(BODY, b)
            sequence(TAIL, B - 1)

        @block.tensor
        def _(pe):
            pe.wait_ge(set_pool, 6)
            pe.wait_ge(set_dve, 1)
            nc.tensor.matmul(bank[0][:, 0:1], ones[:, :], small[:, 0:1], start=True, stop=True).then_inc(ring_full, 1)
            pe.wait_ge(set_dve, 6)
            for k in range(KC):
                if k == KC - 1:
                    pe.wait_ge(ring_free, 1)
                for o in range(KC):
                    t = nc.tensor.transpose(bank[(1 + k) % RING][:, P * o:P * o + P], prob[:, 1, o, P * k:P * k + P],
                                            ident[:, :])
                t.then_inc(ring_full, 1)
            pe.wait_ge(set_dve, 6 + KC)
            pe.wait_ge(set_wo, 16)
            pe.wait_ge(ring_free, 2)
            for k in range(KC):
                m = nc.tensor.matmul(bank[5 % RING][:, :], o32[:, 0, P * k:P * k + P], v[:, k, :], start=(k == 0),
                                     stop=(k == KC - 1))
                if k == 0:
                    m.then_inc(step_used, 2)
            m.then_inc(ring_full, 1)

            def products(o, u, left, right):
                terms = [(k, x, y) for k in range(KC) for x, y in ((HI, HI), (LO, HI), (HI, LO))]
                for n, (k, x, y) in enumerate(terms):
                    m = nc.tensor.matmul(ring(o, u)[:, :], left(x, k), right(y, k), start=(n == 0),
                                         stop=(n == len(terms) - 1))
                m.then_inc(ring_full, 1)

            def use(o, b, u):
                kind = u[0]
                pe.wait_ge(ring_free, used(o, b, u) - RING)
                if kind in ("T1", "T2", "T3"):
                    l, t = int(kind[1]) - 1, u[1]
                    pe.wait_ge(hn_done[l], tile(b if l == 2 else b + 1, t))
                    for k in range(KC):
                        m = nc.tensor.transpose(ring(o, u)[:, P * k:P * k + P], hn[:, l, P * k:P * k + P],
                                                ident[:, :])
                    m.then_inc(ring_full, 1)
                elif kind in ("F1", "F2"):
                    t = u[1]
                    pe.wait_ge(ring_free, used(o, b, ("T" + ("1" if kind == "F1" else "3"), t)))
                    for k in range(KC):
                        for part in (HI, LO):
                            m = nc.tensor.matmul(ring(o, u)[:, :], hts[:, (kind == "F2") * 1, part, k, :], wfT[:, k, :],
                                                 start=(k == 0 and part == HI), stop=(k == KC - 1 and part == LO))
                    m.then_inc(ring_full, 1)
                elif kind == "V":
                    t = u[1]
                    pe.wait_ge(ring_free, used(o, b, ("T2", t)))
                    pe.wait_ge(w_split, wsplit(o, b, ("WV", KC - 1)))
                    products(o, u, lambda x, k: hT[:, x, k, P * t:P * t + P], lambda y, k: wvT[:, y, k, :])
                elif kind == "P":
                    _, g, j, c = u
                    if g == 0:
                        pe.wait_ge(ring_free, used(o, b, ("T2", QPC * c + QPC - 1)))
                        pe.wait_ge(w_split, wsplit(o, b, ("QK", g, j)))
                    elif g == 1:
                        pe.wait_ge(w_split, b * W + FIRST_W)
                    else:
                        pe.wait_ge(w_split, wsplit(o, b, ("QK", g, j)))
                    products(o, u, lambda x, k: wqk[:, x, j, k, :], lambda y, k: hT[:, y, k, CW * c:CW * c + CW])
                elif kind == "A":
                    _, g, h, qb, kc = u
                    c, r = qb // QPC, qb % QPC
                    if h == 0 and r == 0 and kc == 0:
                        nb = b if g else b + 1
                        pe.wait_ge(stk_in[K_][c], group(nb, g, 32))
                        pe.wait_ge(stk_in[Q_][c], group(nb, g, 32))
                    n = CW if kc < c else max(2 * P, P * (r + 1))
                    nc.tensor.matmul(ring(o, u)[:, 0:n], qst[g % 2][0:KQ, c, h, P * r:P * r + P],
                                     kst[g % 2][0:KQ, kc, h, 0:n], start=True, stop=True).then_inc(ring_full, 1)
                elif kind == "M":
                    _, g, c = u
                    if c == 0:
                        pe.wait_ge(ring_free, used(o, b, maxima(g, 0)[-1]))
                    else:
                        pe.wait_ge(mcol_done, b * GROUPS + (g + 1))
                    nc.tensor.transpose(ring(o, u)[0:4 * QPC, 0:P], mst[:, 0, :] if c == 0 else mcol[:, :], ident[:, :])\
                        .then_inc(ring_full, 1)
                else:
                    t = u[1]
                    pe.wait_ge(w_split, wsplit(o, b, ("WO", KC - 1)))
                    pe.wait_ge(o_split, out_split(b, NCH - 2 + t // QPC))
                    products(o, u, lambda x, k: hT[:, x, k, P * t:P * t + P], lambda y, k: woT[:, y, k, :])

            def scores(b, n, h):
                g, i = n // STEPS, n % STEPS
                c, kb, off = step_of(i)
                off = min(off, 2 * P)
                if h == 0 and kb == 0:
                    pe.wait_ge(mrow_in[c], group(b, g, 32))
                pe.wait_ge(s_exp, exps(b, 4 * n + h - 2))
                nc.tensor.matmul(sbank[h % 2][:, off:CW], kst[g % 2][0:KQ + 2, kb // QPC, h, P * (kb % QPC):P * (kb % QPC) + P],
                                 qst[g % 2][0:KQ + 2, c, h, off:CW], start=True, stop=True).then_inc(s_full, 1)

            def values(b, n):
                g, i = n // STEPS, n % STEPS
                c, kb, off = step_of(i)
                if kb == 0:
                    pe.wait_ge(acc_free, evacuated(b, 2 * g + c - 1))
                if n == 0:
                    pe.wait_ge(ring_free, started(b))
                if diagonal(i):
                    pe.wait_ge(masked, b * NDIAG + (2 * QPC * g + i % QPC + (QPC if c else 0) + 1))
                else:
                    pe.wait_ge(s_exp, exps(b, 4 * n + 3))
                for h in range(4):
                    nc.tensor.matmul(accv[HD * h:HD * h + HD, off:CW], v[:, kb, P * g + HD * h:P * g + HD * h + HD],
                                     prob[:, n % 2, h, off:CW], start=(kb == 0), stop=(kb == QPC * (c + 1) - 1))

            def sums(b, n):
                c, kb, off = step_of(n % STEPS)
                for h in range(4):
                    m = nc.tensor.matmul(accs[HD * h:HD * h + HD, off:CW], ones[:, 0:HD], prob[:, n % 2, h, off:CW],
                                         start=(kb == 0), stop=(kb == QPC * (c + 1) - 1))
                m.then_inc(step_used, 1)

            def sequence(o, b):
                for n in range(NSTEP):
                    g, i = n // STEPS, n % STEPS
                    first, second = filler(g, i)
                    if g == GROUPS - 1 and i >= STEPS - FIRST_SLOT:
                        first, second = o.slots[i - STEPS + FIRST_SLOT], []
                    scores(b, n, 0)
                    scores(b, n, 1)
                    for u in first:
                        use(o, b, u)
                    if n:
                        values(b, n - 1)
                    scores(b, n, 2)
                    scores(b, n, 3)
                    for u in second:
                        use(o, b, u)
                    if n:
                        sums(b, n - 1)
                values(b, NSTEP - 1)
                sums(b, NSTEP - 1)
                for q in range(FIRST_SLOT, len(SLOTS)):
                    for u in o.slots[q]:
                        use(o, b, u)

            for q in range(FIRST_SLOT, len(SLOTS)):
                for u in HEAD.slots[q]:
                    use(HEAD, -1, u)
            with pe.Fori(0, B - 1) as b:
                sequence(BODY, b)
            sequence(TAIL, B - 1)


_INS = ["L0_attn_x", "L0_attn_Wqkv", "L0_attn_bqkv", "L0_attn_Wo", "L0_attn_bo", "L0_ffn_weight", "L0_ffn_bias"]
_OUTS = [((4, 1024, 512), "float32")]


def kernel(**inputs):
    import numpy as _np
    import concourse.bacc as _bacc
    from concourse import mybir as _mybir
    from concourse.bass_utils import run_bass_kernel_spmd as _run

    nc = _bacc.Bacc("TRN2", target_bir_lowering=False, num_devices=1)
    arrays, args = {}, []
    for name in _INS:
        a = _np.ascontiguousarray(inputs[name])
        arrays[f"in_{name}_dram"] = a
        args.append(nc.dram_tensor(f"in_{name}_dram", a.shape, _mybir.dt.from_np(a.dtype), kind="ExternalInput").ap())
    for i, (shape, dtype) in enumerate(_OUTS):
        dt = _mybir.dt.from_np(_np.dtype(dtype))
        args.append(nc.dram_tensor(f"out_{i}_dram", shape, dt, kind="ExternalOutput").ap())
    macaron_kernel(nc, *args)
    r = _run(nc, [arrays], core_ids=[0])
    got = tuple(r.results[0][f"out_{i}_dram"] for i in range(len(_OUTS)))
    return got[0]
```

```python
from contextlib import ExitStack

import concourse.bass as bass
from concourse import mybir

F32 = mybir.dt.float32
F32R = mybir.dt.float32r
BF16 = mybir.dt.bfloat16
ALU = mybir.AluOpType
ACT = mybir.ActivationFunctionType
AX = mybir.AxisListType.X

P = 128
B, S, D = 4, 1024, 512
HEADS, HD = 16, 32
TILES = S // P
KC = D // P
GROUPS = HEADS // 4
CW = 512
CHUNKS = S // CW
QPC = CW // P
SCALE = float(HD) ** -0.5
EPS_LN = 1e-5
EPS_FFN = 1e-10
NEG = -1e30
KQ = 3 * HD
HI, LO = 0, 1
K_, Q_ = 0, 1
W_COLUMN = {K_: D, Q_: 0}

RING = 4
STEPS = QPC + 2 * QPC


def step_of(i):
    c, kb = (0, i) if i < QPC else (1, i - QPC)
    return c, kb, max(0, P * kb - CW * c)


def diagonal(i):
    c, kb, _ = step_of(i)
    return kb >= QPC * c


def maxima(g, c):
    return [("A", g, h, QPC * c + r, kc) for h in range(4) for r in range(QPC) for kc in range(c + 1)]


def pieces(g):
    return [("P", g, K_, 0), ("P", g, Q_, 0), ("P", g, K_, 1), ("P", g, Q_, 1)]


AHEAD = 24
AHEAD_0 = 24


def share(work, n, i):
    part = work[len(work) * i // n:len(work) * (i + 1) // n]
    return part[:(len(part) + 1) // 2], part[(len(part) + 1) // 2:]


def filler(g, i):
    first, second = [], []
    if i < 2:
        first, second = share(maxima(g, 1)[AHEAD if g else AHEAD_0:], 2, i)
    elif i == 2:
        first = [("M", g, 1)]
    if g + 1 == GROUPS:
        if i >= STEPS - FIRST_SLOT:
            return SLOTS[i - STEPS + FIRST_SLOT], []
        return first, second
    if i < 4:
        return first + second, [pieces(g + 1)[i]]
    first, second = share(maxima(g + 1, 0) + maxima(g + 1, 1)[:AHEAD], STEPS - 4, i - 4)
    return first, second + ([("M", g + 1, 0)] if i == 8 else [])


def norm_parts(g, i):
    if i <= QPC:
        return 2 * g - 1, [i - 1] if g and i else []
    per = 2 if g + 1 == GROUPS else 1
    return 2 * g, [n for n in range(per * (i - QPC - 1), per * (i - QPC)) if n < 4]


def between():
    plan = [
        "O.0 O.1",
        "O.2 O.3",
        "T3.0",
        "F2.0 T3.1",
        "",
        "F2.1 T3.2",
        "F2.2 T3.3",
        "F2.3 T1.0",
        "O.4 F1.0 T1.1",
        "O.5 F1.1 T3.4 T1.2",
        "O.6 F2.4 F1.2 T3.5 T1.3 T2.0",
        "",
        "",
        "",
        "",
        "",
        "O.7 F2.5 F1.3 T3.6",
        "T2.1",
        "",
        "",
        "F2.6 T3.7 T2.2",
        "V.0 T2.3 V.1 F2.7 T1.4",
        "",
        "F1.4 T1.5",
        "P",
        "",
        "F1.5 T1.6 P",
        "V.2 F1.6 T1.7 T2.4",
        "V.3 F1.7",
        "A T2.5 A V.4",
        "T2.6 A V.5",
        "A T2.7 A*5 P A*4 P A*3",
        "M V.6 V.7 A*7",
        "A*3",
        "A*2",
        "A*12",
    ]
    nxt = {"P": iter(pieces(0)), "M": iter([("M", 0, 0)]), "A": iter(maxima(0, 0) + maxima(0, 1)[:AHEAD_0])}
    slots = []
    for row in plan:
        slots.append([])
        for word in row.split():
            kind, _, times = word.partition("*")
            if kind in nxt:
                slots[-1] += [next(nxt[kind]) for _ in range(int(times or 1))]
            else:
                kind, t = word.split(".")
                slots[-1].append((kind, int(t)))
    assert not any(list(rest) for rest in nxt.values())
    return slots


SLOTS = between()
EARLY = (0, 1, 2, 3)
FIRST_SLOT = 4
LAST_NORM = FIRST_SLOT + 1
ENDING = ("O", "T3", "F2")


OUT_SPLITS = {(2, 3): [0], (2, 5): [1], (2, 6): [2], (2, 7): [3], (2, 9): [4], (3, 5): [5], (3, 7): [6]}


class Order:

    def __init__(self, uses, slots, before, split_before):
        self.slots, self.before, self.split_before = slots, before, split_before
        self.uses = uses
        self.at = {u: n for n, u in enumerate(uses)}
        self.split = {u: n for n, u in enumerate([u for u in uses if u[0] in ("T1", "T2", "T3", "P", "M")])}
        assert len(self.at) == len(uses)

    def next(self, q):
        return self.slots[q + 1] if q + 1 < len(self.slots) else []


def flat(slots):
    return [u for s in slots for u in s]


SETUP_USES = 6
GROUP_USES = [u for g in range(GROUPS) for i in range(STEPS) for part in filler(g, i) for u in part]
HEAD = Order(flat([[u for u in s if u[0] not in ENDING] for s in SLOTS[FIRST_SLOT:]]),
             [[u for u in s if u[0] not in ENDING] for s in SLOTS], SETUP_USES, 0)
_BASE, _SPLIT = SETUP_USES + len(HEAD.uses), len(HEAD.split)
BODY = Order(GROUP_USES + flat(SLOTS[FIRST_SLOT:]), SLOTS, _BASE, _SPLIT)
TAIL = Order(GROUP_USES + flat([[u for u in s if u[0] in ENDING] for s in SLOTS[FIRST_SLOT:]]),
             [[u for u in s if u[0] in ENDING] for s in SLOTS], _BASE, _SPLIT)
R, NSPLIT = len(BODY.uses), len(BODY.split)
assert R % RING == 0

NEXT_W = [("WV", k) for k in range(KC)] + [("QK", g, j) for g in (0, 1) for j in (K_, Q_)]
WCHUNKS = [("QK", g, j) for g in (2, 3) for j in (K_, Q_)] + [("WO", g) for g in range(KC)] + NEXT_W
W, FIRST_W = len(WCHUNKS), len(NEXT_W)
WAT = {w: FIRST_W + n for n, w in enumerate(WCHUNKS)}
_P0 = [q for q, s in enumerate(SLOTS) if pieces(0)[-1] in s][0]
SPLIT_SLOTS = {4: NEXT_W[0], 5: NEXT_W[1], 6: NEXT_W[2], 7: NEXT_W[3], 8: NEXT_W[4], 9: NEXT_W[5],
               _P0 + 1: NEXT_W[6], _P0 + 2: NEXT_W[7]}
SPLIT_STEPS = {(0, 4): WCHUNKS[0], (0, 5): WCHUNKS[1], (1, 4): WCHUNKS[2], (1, 5): WCHUNKS[3],
               (3, 0): WCHUNKS[4], (3, 1): WCHUNKS[5], (3, 2): WCHUNKS[6], (3, 4): WCHUNKS[7]}
LOAD_SLOTS = {4: NEXT_W[2], 5: NEXT_W[3], 6: NEXT_W[4], 7: NEXT_W[5], 8: NEXT_W[6], 9: NEXT_W[7]}
LOAD_STEPS = {(0, 1): WCHUNKS[0], (0, 2): WCHUNKS[1], (1, 1): WCHUNKS[2], (1, 2): WCHUNKS[3],
              (2, 1): WCHUNKS[4], (2, 2): WCHUNKS[5], (3, 0): WCHUNKS[6], (3, 3): WCHUNKS[7],
              (3, 5): NEXT_W[0], (3, 6): NEXT_W[1]}
NS = 4 * STEPS * GROUPS
NSTEP = STEPS * GROUPS
NDIAG = 2 * QPC * GROUPS
NCH = CHUNKS * GROUPS


def macaron_kernel(nc, x, wqkv, bqkv, wo, bo, wf, bf, out):
    with ExitStack() as ctx:
        def sb(name, shape, dt=F32):
            return ctx.enter_context(nc.sbuf_tensor(name, shape, dt))

        def sem(name):
            return ctx.enter_context(nc.semaphore(name))

        xt = sb("xt", [P, TILES, D])
        wfT = sb("wfT", [P, KC, D], F32R)
        wqk = sb("wqk", [P, 2, 2, KC, P], F32R)
        stage = sb("stage", [P, 2, D])
        hT = sb("hT", [P, 2, KC, S], F32R)
        hts = sb("hts", [P, 2, 2, KC, P], F32R)
        hn = sb("hn", [P, 3, D])
        v = sb("v", [P, TILES, D])
        nat = sb("nat", [P, 2, 2, CW], F32R)
        kst = [sb(f"kst{n}", [P, CHUNKS, 4, CW], F32R) for n in range(2)]
        qst = [sb(f"qst{n}", [P, CHUNKS, 4, CW], F32R) for n in range(2)]
        prob = sb("prob", [P, 2, 4, CW])
        o32 = sb("o32", [P, 4, CW])
        rec = sb("rec", [P, CW])
        junk = sb("junk", [P, 2, CW], BF16)
        mask = sb("mask", [P, CW], BF16)
        ident = sb("ident", [P, P])
        ones = sb("ones", [P, P])
        hb = sb("hb", [P, D])
        bo2 = sb("bo2", [P, D])
        bqk = sb("bqk", [P, 3 * KC])
        small = sb("small", [P, 8])
        st6 = sb("st6", [P, 3, 2, 6])
        mv = sb("mv", [P, 3, TILES, 2])
        ve = sb("ve", [P, 3, TILES])
        rstd = sb("rstd", [P, 3, TILES])
        nmr = sb("nmr", [P, 3, TILES])
        mst = sb("mst", [P, 3, 4 * QPC])
        mcol = sb("mcol", [P, 4 * QPC])
        mrow = sb("mrow", [4 * QPC, 2, 2, P], F32R)
        scr = nc.dram_tensor("stack_scratch", [2, CHUNKS, 2, HD, 4, CW], F32, kind="Internal").ap()

        wvT, woT = qst[1], qst[0]
        bank = [ctx.enter_context(nc.psum_tensor(f"bank{n}", [P, CW], F32)) for n in range(8)]
        sbank, accv, accs = bank[4:6], bank[6], bank[7]

        ring_full, ring_free = sem("ring_full"), sem("ring_free")
        hi_done = sem("hi_done")
        s_full, s_exp = sem("s_full"), sem("s_exp")
        masked, step_used = sem("masked"), sem("step_used")
        value_done = sem("value_done")
        accv_free, acc_free = sem("accv_free"), sem("acc_free")
        rec_done, norm_done = sem("rec_done"), sem("norm_done")
        o_hi, o_split = sem("o_hi"), sem("o_split")
        w_hi, w_split = sem("w_hi"), sem("w_split")
        st_done = [sem(f"st_done{n}") for n in range(3)]
        mv_done = [sem(f"mv_done{n}") for n in range(3)]
        ve_done = [sem(f"ve_done{n}") for n in range(3)]
        rs_done = [sem(f"rs_done{n}") for n in range(3)]
        nm_done = [sem(f"nm_done{n}") for n in range(3)]
        hn_done = [sem(f"hn_done{n}") for n in range(3)]
        xb_done = [sem(f"xb_done{n}") for n in range(3)]
        mcol_done = sem("mcol_done")
        x_in = [sem(f"x_in{t}") for t in range(TILES)]
        x_out = [sem(f"x_out{t}") for t in range(TILES)]
        staged = [sem(f"staged{n}") for n in range(2)]
        scr_in = sem("scr_in")
        stk_in = [[sem(f"stk_in{j}{c}") for c in range(CHUNKS)] for j in range(2)]
        mrow_in = [sem(f"mrow_in{c}") for c in range(CHUNKS)]
        set_wf, set_wo, set_b = sem("set_wf"), sem("set_wo"), sem("set_b")
        set_pool, set_dve = sem("set_pool"), sem("set_dve")

        def used(o, b, u):
            return (0 if o is HEAD else b * R) + (o.before + o.at[u] + 1)

        def started(b):
            return b * R + BODY.before

        def split(o, b, u):
            return (0 if o is HEAD else b * NSPLIT) + (o.split_before + o.split[u] + 1)

        def ring(o, u):
            return bank[(o.before + o.at[u]) % RING][:, :]

        def tile(b, t):
            return b * TILES + (t + 1)

        def exps(b, n):
            return b * NS + (n + 3)

        def stepped(b, n):
            return b * NSTEP + (n + 3)

        def evacuated(b, n):
            return b * NCH + (n + 2)

        def normed(b, n):
            return b * NCH + (n + 2)

        def out_split(b, n):
            return b * NCH + (n + 5)

        def wsplit(o, b, w):
            return NEXT_W.index(w) + 1 if o is HEAD else b * W + (WAT[w] + 1)

        def group(b, g, per):
            return b * (GROUPS * per) + per * (g + 1)

        def source(w):
            if w[0] == "QK":
                at = W_COLUMN[w[2]] + P * w[1]
                return wqkv[:, at:at + P].rearrange("(k p) n -> p k n", p=P)
            if w[0] == "WO":
                return wo[P * w[1]:P * w[1] + P, :]
            return wqkv[P * w[1]:P * w[1] + P, 2 * D:3 * D]

        def target(w, part):
            if w[0] == "QK":
                return wqk[:, part, w[2], :, :].rearrange("p k n -> p (k n)")
            return (woT if w[0] == "WO" else wvT)[:, part, w[1], :]

        def stage_as(w, n):
            return stage[:, n, :].rearrange("p (k n) -> p k n", k=KC) if w[0] == "QK" else stage[:, n, :]

        def blocks(o, u):
            return ring(o, u).rearrange("p (k n) -> p k n", k=KC)

        def bias_of(j, g):
            return bqk[:, KC * (j == K_) + g:KC * (j == K_) + g + 1]

        dve_past, pool_past, sp_past = sem("dve_past"), sem("pool_past"), sem("sp_past")
        block = ctx.enter_context(nc.Block())

        @block.sync
        def _(sp):
            sp.dma_start(prob[:, 0, :, :], wf.rearrange("(k p) n -> p k n", p=P)).then_inc(set_wf, 16)
            sp.dma_start(xt[:, 0, :], x[0, 0:P, :]).then_inc(x_in[0], 16)
            sp.dma_start(hb[:, :], bf.partition_broadcast(P)).then_inc(set_b, 16)
            sp.dma_start(bo2[:, :], bo.partition_broadcast(P)).then_inc(set_b, 16)
            sp.dma_start(bqk[:, :], bqkv.rearrange("(k p) -> p k", p=P), allow_slow_non_contiguous=True).then_inc(set_b, 16)
            sp.dma_start(v[:, 0:KC, :], wo.rearrange("(k p) n -> p k n", p=P)).then_inc(set_wo, 16)
            for t in range(1, TILES):
                sp.dma_start(xt[:, t, :], x[0, P * t:P * t + P, :]).then_inc(x_in[t], 16)
            def load_weights(o, b, w):
                n = wsplit(o, b, w) - 1
                slot = (NEXT_W.index(w) if o is HEAD else WAT[w]) % 2
                if o is not HEAD or NEXT_W.index(w) >= 2:
                    sp.wait_ge(w_split, n - 1)
                sp.dma_start(stage_as(w, slot), source(w)).then_inc(staged[slot], 16)

            def stack(o, b, u, first_free):
                _, g, j, c = u
                nb = b if o.at[u] < len(GROUP_USES) and o is not HEAD else b + 1
                lay = scr[j, c]
                if first_free is not None:
                    sp.wait_ge(s_full, first_free)
                    sp.sem_inc(sp_past, 1)
                sp.wait_ge(hi_done, split(o, b, u))
                sp.dma_start(lay[HI].rearrange("r h n -> h r n"), nat[:, j, HI, :].bitcast(F32)).then_inc(scr_in, 16)
                sp.wait_ge(ring_free, used(o, b, u))
                sp.dma_start(lay[LO].rearrange("r h n -> h r n"), nat[:, j, LO, :].bitcast(F32)).then_inc(scr_in, 16)
                n = pieces(g).index(u)
                sp.wait_ge(scr_in, nb * (GROUPS * 128) + (128 * g + 32 * (n + 1)))
                both = lay.rearrange("l r h n -> (l r) h n")
                dst = (kst, qst)[j][g % 2]
                pair, single = ((0, 2 * HD), (2 * HD, KQ)) if j == K_ else ((HD, KQ), (0, HD))
                sp.dma_start(dst[pair[0]:pair[1], c, :, :].bitcast(F32), both).then_inc(stk_in[j][c], 16)
                sp.dma_start(dst[single[0]:single[1], c, :, :].bitcast(F32), both[0:HD]).then_inc(stk_in[j][c], 16)

            def rows(o, b, u):
                _, g, c = u
                sp.wait_ge(ring_free, used(o, b, u))
                for part in (HI, LO):
                    row = KQ + part
                    sp.dma_start(qst[g % 2][row:row + 1, c, :, :].rearrange("p h n -> p (h n)").bitcast(F32),
                                 mrow[:, c, part, :].bitcast(F32)).then_inc(mrow_in[c], 16)

            def event(o, b, u):
                if u[0] == "P":
                    stack(o, b, u, b * NS + 4 * STEPS * (u[1] - 1) if u[1] >= 2 else None)
                elif u[0] == "M":
                    rows(o, b, u)
                elif u[0] == "F2":
                    t = u[1]
                    sp.wait_ge(ring_free, used(o, b, u))
                    sp.sem_inc(sp_past, 1)
                    sp.dma_start(out[b, P * t:P * t + P, :], xt[:, t, :]).then_inc(x_out[t], 16)

            def slot(o, b, q):
                if o is BODY and q:
                    for u in o.slots[q - 1]:
                        if u[0] == "F2":
                            t = u[1]
                            sp.wait_ge(x_out[t], b * 16 + 16)
                            sp.sem_inc(sp_past, 1)
                            sp.dma_start(xt[:, t, :], x[b + 1, P * t:P * t + P, :]).then_inc(x_in[t], 16)
                for u in o.slots[q]:
                    event(o, b, u)
                if o is not TAIL and q in LOAD_SLOTS:
                    load_weights(o, b, LOAD_SLOTS[q])

            def sequence(o, b):
                for g in range(GROUPS):
                    for i in range(STEPS):
                        if g == GROUPS - 1 and i >= STEPS - FIRST_SLOT:
                            slot(o, b, i - STEPS + FIRST_SLOT)
                        else:
                            for part in filler(g, i):
                                for u in part:
                                    event(o, b, u)
                        if (g, i) in LOAD_STEPS and not (o is TAIL and LOAD_STEPS[g, i] in NEXT_W):
                            load_weights(o, b, LOAD_STEPS[g, i])
                for q in range(FIRST_SLOT, len(SLOTS)):
                    slot(o, b, q)

            for w in NEXT_W[0:2]:
                load_weights(HEAD, -1, w)
            for q in range(FIRST_SLOT, len(SLOTS)):
                slot(HEAD, -1, q)
            with sp.Fori(0, B - 1) as b:
                sequence(BODY, b)
            sequence(TAIL, B - 1)
            for t in range(TILES):
                sp.wait_ge(x_out[t], 16 * B)

        @block.gpsimd
        def _(pool):
            nc.gpsimd.memset(ident[:, :], 0.0).then_inc(set_pool, 1)
            nc.gpsimd.memset(mask[:, :], 0.0).then_inc(set_pool, 1)
            nc.gpsimd.memset(ones[:, :], 1.0).then_inc(set_pool, 1)
            nc.gpsimd.memset(small[:, 4:5], -0.5).then_inc(set_pool, 1)
            pool.wait_ge(set_pool, 4)
            nc.gpsimd.affine_select(out=ident[:, :], in_=ident[:, :], compare_op=ALU.not_equal, fill=1.0, base=0,
                                    pattern=[[-1, P]], channel_multiplier=1).then_inc(set_pool, 1)
            nc.gpsimd.affine_select(out=mask[:, CW - P:CW], in_=mask[:, CW - P:CW], compare_op=ALU.is_ge, fill=NEG,
                                    base=0, pattern=[[-1, P]], channel_multiplier=1).then_inc(set_pool, 1)
            pool.wait_ge(set_pool, 6)
            for n in range(2):
                nc.gpsimd.memset(kst[n][KQ:KQ + 2, :, :, :].bitcast(F32), 1.0).then_inc(set_pool, 1)
            pool.wait_ge(set_pool, 8)
            pool.wait_ge(set_b, 48)
            nc.gpsimd.tensor_scalar(hb[:, :], hb[:, :], 0.5, 0.0, ALU.mult, ALU.add).then_inc(o_split, 4)
            pool.wait_ge(o_split, 4)

            def weights(o, b, w):
                slot = (NEXT_W.index(w) if o is HEAD else WAT[w]) % 2
                pool.wait_ge(w_hi, wsplit(o, b, w))
                nc.gpsimd.tensor_tensor(target(w, LO), stage[:, slot, :], target(w, HI).bitcast(F32), ALU.subtract)\
                    .then_inc(w_split, 1)

            def rsqrt(b, l, t):
                pool.wait_ge(mv_done[l], tile(b, t))
                pool.sem_inc(pool_past, 1)
                nc.gpsimd.tensor_scalar(ve[:, l, t:t + 1], mv[:, l, t, 1:2], 1.0, EPS_LN, ALU.mult, ALU.add)\
                    .then_inc(ve_done[l], 1)
                pool.wait_ge(ve_done[l], tile(b, t))
                nc.gpsimd.tensor_tensor(rstd[:, l, t:t + 1], ve[:, l, t:t + 1], small[:, 4:5], ALU.pow)\
                    .then_inc(rs_done[l], 1)

            def add_bias(b, l, t):
                pool.wait_ge(hn_done[l], tile(b, t))
                nc.gpsimd.tensor_tensor(xt[:, t, :], xt[:, t, :], (bo2 if l == 1 else hb)[:, :], ALU.add)\
                    .then_inc(xb_done[l], 1)

            def split_output(b, n):
                g, c = n // CHUNKS, n % CHUNKS
                hi, lo = (hT[:, part, g, CW * c:CW * c + CW] for part in (HI, LO))
                pool.wait_ge(o_hi, b * NCH + (n + 1))
                nc.gpsimd.tensor_tensor(lo, o32[:, n % 4, :], hi.bitcast(F32), ALU.subtract).then_inc(o_split, 1)

            def step(b, g, i):
                if diagonal(i):
                    n = STEPS * g + i
                    off = step_of(i)[2]
                    pool.wait_ge(s_exp, exps(b, 4 * n + 3))
                    part = prob[:, n % 2, :, off:off + P]
                    pool.sem_inc(pool_past, 1)
                    nc.gpsimd.affine_select(out=part, in_=part, compare_op=ALU.is_ge, fill=0.0, base=0,
                                            pattern=[[0, 4], [1, P]], channel_multiplier=-1).then_inc(masked, 1)

            def slot(o, b, q):
                now, after = o.slots[q], o.next(q)
                for kind, t in [u for u in now if u[0] in ("F1", "O")]:
                    rsqrt(*((b + 1, 1) if kind == "F1" else (b, 2)), t)
                for t in [u[1] for u in after if u[0] == "T1"]:
                    rsqrt(b + 1, 0, t)
                for kind, t in [u for u in now if u[0] in ("T1", "T2", "T3")]:
                    l = int(kind[1]) - 1
                    add_bias(b if l == 2 else b + 1, l, t)
                if o is not TAIL and q in SPLIT_SLOTS:
                    weights(o, b, SPLIT_SLOTS[q])
                if q == LAST_NORM and o is not HEAD:
                    split_output(b, 7)

            def sequence(o, b):
                for g in range(GROUPS):
                    for i in range(STEPS):
                        step(b, g, i)
                        for n in OUT_SPLITS.get((g, i), []):
                            split_output(b, n)
                        if (g, i) in SPLIT_STEPS:
                            weights(o, b, SPLIT_STEPS[g, i])
                        if g == GROUPS - 1 and i >= STEPS - FIRST_SLOT:
                            slot(o, b, i - STEPS + FIRST_SLOT)
                for q in range(FIRST_SLOT, len(SLOTS)):
                    slot(o, b, q)

            for q in range(FIRST_SLOT, len(SLOTS)):
                slot(HEAD, -1, q)
            with pool.Fori(0, B - 1) as b:
                sequence(BODY, b)
            sequence(TAIL, B - 1)

        @block.vector
        def _(dve):
            def filled(n):
                return dve.wait_ge(ring_full, n)

            wn, wt = prob[:, 0, :, :], prob[:, 1, :, :]
            dve.wait_ge(set_wf, 16)
            nc.vector.tensor_reduce(small[:, 0:1], wn.rearrange("p k n -> p (k n)"), AX, ALU.add,
                                    apply_absolute_value=True).then_inc(set_dve, 1)
            filled(1)
            nc.vector.tensor_scalar(small[:, 1:2], bank[0][:, 0:1], 1.0 / (D * D), None, ALU.mult).then_inc(ring_free, 1)
            dve.wait_ge(ring_free, 1)
            nc.vector.tensor_scalar(small[:, 2:3], small[:, 1:2], EPS_FFN, 0.5, ALU.add, ALU.mult).then_inc(set_dve, 1)
            nc.vector.tensor_scalar(small[:, 5:6], small[:, 1:2], 0.5, None, ALU.mult).then_inc(set_dve, 1)
            dve.wait_ge(set_dve, 3)
            nc.vector.tensor_scalar(small[:, 3:4], small[:, 2:3], -1.0, None, ALU.mult).then_inc(set_dve, 1)
            dve.wait_ge(set_dve, 4)
            flat = [a.rearrange("p k n -> p (k n)") for a in (wn, wt)]
            nc.vector.tensor_scalar(flat[1], flat[0], small[:, 3:4], None, ALU.is_lt).then_inc(set_dve, 1)
            dve.wait_ge(set_dve, 5)
            nc.vector.scalar_tensor_tensor(flat[1], flat[0], small[:, 2:3], flat[1], ALU.is_gt, ALU.subtract)\
                .then_inc(set_dve, 1)
            dve.wait_ge(set_b, 48)
            dve.wait_ge(set_pool, 6)
            for k in range(KC):
                nc.vector.tensor_scalar(o32[:, 0, P * k:P * k + P], ones[:, :], bqk[:, 2 * KC + k:2 * KC + k + 1], None,
                                        ALU.mult).then_inc(set_dve, 1)
            nc.vector.memset(rec[:, :], 0.0).then_inc(norm_done, 1)
            dve.wait_ge(norm_done, 1)
            for k in range(KC):
                filled(2 + k)
                nc.vector.tensor_copy(wfT[:, k, :], bank[(1 + k) % RING][:, :]).then_inc(ring_free, 1)
            filled(6)
            nc.vector.tensor_tensor(bo2[:, :], bank[5 % RING][:, :], bo2[:, :], ALU.add).then_inc(ring_free, 1)

            def stats(o, run, b, l, t):
                if l == 0:
                    dve.wait_ge(x_in[t], b * 16 + 16)
                else:
                    dve.wait_ge(ring_free, used(o, run, (("F1", "O")[l - 1], t)))
                s = st6[:, l, t % 2, :]
                nc.vector.bn_stats(s, xt[:, t, :]).then_inc(st_done[l], 1)
                dve.wait_ge(st_done[l], tile(b, t))
                dve.sem_inc(dve_past, 1)
                nc.vector.bn_aggr(mv[:, l, t, :], s).then_inc(mv_done[l], 1)

            def shift(b, l, t):
                dve.wait_ge(rs_done[l], tile(b, t))
                nc.vector.scalar_tensor_tensor(nmr[:, l, t:t + 1], mv[:, l, t, 0:1], -1.0, rstd[:, l, t:t + 1],
                                               ALU.mult, ALU.mult).then_inc(nm_done[l], 1)

            def low(o, b, u, dst, src, hi, first=None):
                dve.wait_ge(hi_done, split(o, b, u))
                if first is None:
                    i = nc.vector.tensor_tensor(dst, src, hi.bitcast(F32), ALU.subtract)
                else:
                    i = nc.vector.scalar_tensor_tensor(dst, src, first[0], hi.bitcast(F32), first[1], ALU.subtract)
                i.then_inc(ring_free, 1)

            def residual(o, b, u, nb, l):
                t = u[1]
                dve.wait_ge(ring_full, used(o, b, u))
                dve.wait_ge(xb_done[l], tile(nb, t))
                if l == 1:
                    nc.vector.tensor_tensor(xt[:, t, :], ring(o, u), xt[:, t, :], ALU.add).then_inc(ring_free, 1)
                else:
                    nc.vector.scalar_tensor_tensor(xt[:, t, :], ring(o, u), small[:, 5:6], xt[:, t, :],
                                                   ALU.mult, ALU.add).then_inc(ring_free, 1)

            def maximum(o, b, u):
                _, g, h, qb, kc = u
                c, r = qb // QPC, qb % QPC
                dve.wait_ge(ring_full, used(o, b, u))
                at = 4 * h + r
                if kc < c:
                    nc.vector.tensor_reduce(mst[:, 1, at:at + 1], ring(o, u), AX, ALU.max).then_inc(ring_free, 1)
                else:
                    n = P * (r + 1)
                    dve.wait_ge(ring_free, used(o, b, u) - 2)
                    dve.sem_inc(dve_past, 1)
                    nc.vector.tensor_tensor_reduce(junk[:, o.at[u] % 2, 0:n], ring(o, u)[:, 0:n], mask[:, CW - n:CW],
                                                   1.0, -3e38, ALU.add, ALU.max, mst[:, 2 * c, at:at + 1])\
                        .then_inc(ring_free, 1)
                if u == maxima(g, 1)[-1]:
                    dve.wait_ge(ring_free, used(o, b, u))
                    nc.vector.tensor_tensor(mcol[:, :], mst[:, 1, :], mst[:, 2, :], ALU.max).then_inc(mcol_done, 1)

            def invert(b, n, part):
                if part == 0:
                    dve.wait_ge(acc_free, evacuated(b, n))
                at = slice(P * part, P * part + P)
                nc.vector.reciprocal(rec[:, at], rec[:, at]).then_inc(rec_done, 1)

            def normalise(b, n):
                dve.wait_ge(rec_done, b * (4 * NCH) + 4 * (n + 1))
                nc.vector.tensor_tensor(o32[:, n % 4, :], o32[:, n % 4, :], rec[:, :], ALU.mult).then_inc(norm_done, 1)

            def use(o, b, u):
                if u[0] == "A":
                    maximum(o, b, u)
                elif u[0] == "V":
                    dve.wait_ge(ring_full, used(o, b, u))
                    nc.vector.tensor_copy(v[:, u[1], :], ring(o, u)).then_inc(ring_free, 1)
                elif u[0] == "P":
                    _, g, j, c = u
                    low(o, b, u, nat[:, j, LO, :], ring(o, u), nat[:, j, HI, :], (bias_of(j, g), ALU.add))
                elif u[0] == "M":
                    c = u[2]
                    low(o, b, u, mrow[:, c, LO, :], ring(o, u)[0:4 * QPC, 0:P], mrow[:, c, HI, :], (-1.0, ALU.mult))
                elif u[0] == "T2":
                    at = slice(P * u[1], P * u[1] + P)
                    low(o, b, u, hT[:, LO, :, at], blocks(o, u), hT[:, HI, :, at])
                elif u[0] in ("T1", "T3"):
                    which = (u[0] == "T3") * 1
                    low(o, b, u, hts[:, which, LO, :, :], blocks(o, u), hts[:, which, HI, :, :])
                else:
                    residual(o, b, u, *{"F1": (b + 1, 0), "O": (b, 1), "F2": (b, 2)}[u[0]])

            def slot(o, b, q):
                parts = [2 * (q - FIRST_SLOT), 2 * (q - FIRST_SLOT) + 1] \
                    if o is not HEAD and FIRST_SLOT <= q <= LAST_NORM else []
                for u in o.slots[q]:
                    use(o, b, u)
                    if u[0] == "F1":
                        stats(o, b, b + 1, 1, u[1])
                    if u[0] == "O":
                        stats(o, b, b, 2, u[1])
                    if len(parts) == 2:
                        invert(b, NCH - 1, parts.pop(0))
                for part in parts:
                    invert(b, NCH - 1, part)
                if o is not HEAD and q == LAST_NORM:
                    normalise(b, NCH - 1)
                after = [u[1] for u in o.next(q) if u[0] == "T1"]
                for t in after:
                    stats(o, b, b + 1, 0, t)
                for kind, t in [u for u in o.slots[q] if u[0] in ("F1", "O")]:
                    shift(*((b + 1, 1) if kind == "F1" else (b, 2)), t)
                for t in after:
                    shift(b + 1, 0, t)

            def sequence(o, b):
                for n in range(NSTEP):
                    g, i = n // STEPS, n % STEPS
                    if g == GROUPS - 1 and i >= STEPS - FIRST_SLOT:
                        slot(o, b, i - STEPS + FIRST_SLOT)
                        continue
                    first, second = filler(g, i)
                    for u in first:
                        use(o, b, u)
                    chunk, parts = norm_parts(g, i)
                    for part in parts:
                        invert(b, chunk, part)
                    for u in second:
                        use(o, b, u)
                    if 3 in parts:
                        normalise(b, chunk)
                for q in range(FIRST_SLOT, len(SLOTS)):
                    slot(o, b, q)

            for q in range(FIRST_SLOT, len(SLOTS)):
                slot(HEAD, -1, q)
            with dve.Fori(0, B - 1) as b:
                sequence(BODY, b)
            sequence(TAIL, B - 1)

        @block.scalar
        def _(act):
            act.wait_ge(set_pool, 6)
            nc.scalar.activation(small[:, 6:7], ones[:, 0:1], ACT.Exp).then_inc(s_exp, 2)
            nc.scalar.activation(small[:, 7:8], ones[:, 0:1], ACT.Identity).then_inc(acc_free, 1)
            act.wait_ge(set_b, 48)

            def normal(b, l, t):
                act.wait_ge(nm_done[l], tile(b, t))
                nc.scalar.activation(hn[:, l, :], xt[:, t, :], ACT.Identity, bias=nmr[:, l, t:t + 1],
                                     scale=rstd[:, l, t:t + 1]).then_inc(hn_done[l], 1)

            def high(o, b, u):
                kind = u[0]
                act.wait_ge(ring_full, used(o, b, u))
                if kind == "P":
                    _, g, j, c = u
                    n = pieces(g).index(u)
                    if g or n >= 2:
                        nb = b if g else b + 1
                        act.wait_ge(scr_in, nb * (GROUPS * 128) + (128 * g + 32 * (n - 1)))
                    i = nc.scalar.activation(nat[:, j, HI, :], ring(o, u), ACT.Identity, bias=bias_of(j, g))
                elif kind == "M":
                    i = nc.scalar.activation(mrow[:, u[2], HI, :], ring(o, u)[0:4 * QPC, 0:P], ACT.Identity, scale=-1.0)
                elif kind == "T2":
                    i = nc.scalar.activation(hT[:, HI, :, P * u[1]:P * u[1] + P], blocks(o, u), ACT.Identity)
                else:
                    i = nc.scalar.activation(hts[:, (kind == "T3") * 1, HI, :, :], blocks(o, u), ACT.Identity)
                i.then_inc(hi_done, 1)

            def evacuate(b, n):
                act.wait_ge(o_split, out_split(b, n - 4))
                act.wait_ge(value_done, stepped(b, n // 2 * STEPS + (QPC - 1, STEPS - 1)[n % 2]) - 2)
                nc.scalar.activation(o32[:, n % 4, :], accv[:, :], ACT.Identity).then_inc(accv_free, 1)
                act.wait_ge(step_used, stepped(b, n // 2 * STEPS + (QPC - 1, STEPS - 1)[n % 2]))
                act.wait_ge(norm_done, normed(b, n - 1))
                nc.scalar.activation(rec[:, :], accs[:, :], ACT.Identity).then_inc(acc_free, 1)

            def high_weights(o, b, w):
                n = NEXT_W.index(w) if o is HEAD else WAT[w]
                slot = n % 2
                act.wait_ge(staged[slot], (0 if o is HEAD else b * (W * 8)) + 16 * (n // 2 + 1))
                nc.scalar.activation(target(w, HI), stage[:, slot, :], ACT.Identity).then_inc(w_hi, 1)

            def high_output(b, n):
                g, c = n // CHUNKS, n % CHUNKS
                act.wait_ge(norm_done, normed(b, n))
                nc.scalar.activation(hT[:, HI, g, CW * c:CW * c + CW], o32[:, n % 4, :], ACT.Identity).then_inc(o_hi, 1)

            def slot(o, b, q):
                for u in o.slots[q]:
                    if u in o.split:
                        high(o, b, u)
                for kind, t in [u for u in o.next(q) if u[0] in ("T1", "T2", "T3")]:
                    l = int(kind[1]) - 1
                    normal(b if l == 2 else b + 1, l, t)
                if q == LAST_NORM and o is not HEAD:
                    high_output(b, NCH - 1)
                if o is not TAIL and q in SPLIT_SLOTS:
                    if q == FIRST_SLOT and o is BODY:
                        act.wait_ge(s_full, b * NS + NS)
                    if q == _P0 + 1:
                        act.wait_ge(ring_full, used(o, b, pieces(0)[-1]))
                    high_weights(o, b, SPLIT_SLOTS[q])

            def sequence(o, b):
                for n in range(NSTEP):
                    g, i = n // STEPS, n % STEPS
                    off = step_of(i)[2]
                    act.wait_ge(step_used, stepped(b, n - 2))
                    for h in range(4):
                        act.wait_ge(s_full, b * NS + (4 * n + h + 1))
                        nc.scalar.activation(prob[:, n % 2, h, off:CW], sbank[h % 2][:, off:CW], ACT.Exp, scale=SCALE)\
                            .then_inc(s_exp, 1)
                    if g == GROUPS - 1 and i >= STEPS - FIRST_SLOT:
                        slot(o, b, i - STEPS + FIRST_SLOT)
                    else:
                        for part in filler(g, i):
                            for u in part:
                                if u in o.split:
                                    high(o, b, u)
                    if i == 0 and g:
                        evacuate(b, 2 * g - 1)
                    if i == QPC:
                        evacuate(b, 2 * g)
                    for m in OUT_SPLITS.get((g, i), []):
                        if m == 0:
                            act.wait_ge(ring_full, used(o, b, pieces(3)[-1]))
                        high_output(b, m)
                    if (g, i) in SPLIT_STEPS:
                        if i == 4 and g < 2:
                            act.wait_ge(ring_full, used(o, b, pieces(g + 1)[-1]))
                        if i == 0 and g == 3:
                            act.wait_ge(s_full, b * NS + 3 * 4 * STEPS)
                        high_weights(o, b, SPLIT_STEPS[g, i])
                evacuate(b, NCH - 1)
                for q in range(FIRST_SLOT, len(SLOTS)):
                    slot(o, b, q)

            for q in range(FIRST_SLOT, len(SLOTS)):
                slot(HEAD, -1, q)
            with act.Fori(0, B - 1) as b:
                sequence(BODY, b)
            sequence(TAIL, B - 1)

        @block.tensor
        def _(pe):
            pe.wait_ge(set_pool, 6)
            pe.wait_ge(set_dve, 1)
            nc.tensor.matmul(bank[0][:, 0:1], ones[:, :], small[:, 0:1], start=True, stop=True).then_inc(ring_full, 1)
            pe.wait_ge(set_dve, 6)
            for k in range(KC):
                if k == KC - 1:
                    pe.wait_ge(ring_free, 1)
                for o in range(KC):
                    t = nc.tensor.transpose(bank[(1 + k) % RING][:, P * o:P * o + P], prob[:, 1, o, P * k:P * k + P],
                                            ident[:, :])
                t.then_inc(ring_full, 1)
            pe.wait_ge(set_pool, 8)
            pe.wait_ge(set_dve, 6 + KC)
            pe.wait_ge(set_wo, 16)
            pe.wait_ge(ring_free, 2)
            for k in range(KC):
                m = nc.tensor.matmul(bank[5 % RING][:, :], o32[:, 0, P * k:P * k + P], v[:, k, :], start=(k == 0),
                                     stop=(k == KC - 1))
                if k == 0:
                    m.then_inc(step_used, 2)
            m.then_inc(ring_full, 1)

            def products(o, u, left, right, chunks=range(KC)):
                terms = [(k, x, y) for k in chunks for x, y in ((HI, HI), (LO, HI), (HI, LO))]
                for n, (k, x, y) in enumerate(terms):
                    m = nc.tensor.matmul(ring(o, u)[:, :], left(x, k), right(y, k), start=(k == 0 and n == 0),
                                         stop=(k == KC - 1 and n == len(terms) - 1))
                if KC - 1 in chunks:
                    m.then_inc(ring_full, 1)

            def output(o, b, u, groups):
                t = u[1]
                if groups[0] == 0:
                    pe.wait_ge(ring_free, used(o, b, u) - RING)
                pe.wait_ge(w_split, wsplit(o, b, ("WO", groups[-1])))
                pe.wait_ge(o_split, out_split(b, CHUNKS * groups[-1] + t // QPC))
                products(o, u, lambda x, k: hT[:, x, k, P * t:P * t + P], lambda y, k: woT[:, y, k, :], groups)

            def use(o, b, u):
                kind = u[0]
                if kind == "O":
                    output(o, b, u, [GROUPS - 1] if u[1] in EARLY else list(range(GROUPS)))
                    return
                pe.wait_ge(ring_free, used(o, b, u) - RING)
                if kind in ("T1", "T2", "T3"):
                    l, t = int(kind[1]) - 1, u[1]
                    pe.wait_ge(hn_done[l], tile(b if l == 2 else b + 1, t))
                    for k in range(KC):
                        m = nc.tensor.transpose(ring(o, u)[:, P * k:P * k + P], hn[:, l, P * k:P * k + P],
                                                ident[:, :])
                    m.then_inc(ring_full, 1)
                elif kind in ("F1", "F2"):
                    t = u[1]
                    pe.wait_ge(ring_free, used(o, b, ("T" + ("1" if kind == "F1" else "3"), t)))
                    for k in range(KC):
                        for part in (HI, LO):
                            m = nc.tensor.matmul(ring(o, u)[:, :], hts[:, (kind == "F2") * 1, part, k, :], wfT[:, k, :],
                                                 start=(k == 0 and part == HI), stop=(k == KC - 1 and part == LO))
                    m.then_inc(ring_full, 1)
                elif kind == "V":
                    t = u[1]
                    pe.wait_ge(ring_free, used(o, b, ("T2", t)))
                    pe.wait_ge(w_split, wsplit(o, b, ("WV", KC - 1)))
                    products(o, u, lambda x, k: hT[:, x, k, P * t:P * t + P], lambda y, k: wvT[:, y, k, :])
                elif kind == "P":
                    _, g, j, c = u
                    if g == 0:
                        pe.wait_ge(ring_free, used(o, b, ("T2", QPC * c + QPC - 1)))
                        pe.wait_ge(w_split, wsplit(o, b, ("QK", g, j)))
                    elif g == 1:
                        pe.wait_ge(w_split, b * W + FIRST_W)
                    else:
                        pe.wait_ge(w_split, wsplit(o, b, ("QK", g, j)))
                    products(o, u, lambda x, k: wqk[:, x, j, k, :], lambda y, k: hT[:, y, k, CW * c:CW * c + CW])
                elif kind == "A":
                    _, g, h, qb, kc = u
                    c, r = qb // QPC, qb % QPC
                    if h == 0 and r == 0 and kc == 0:
                        nb = b if g else b + 1
                        pe.wait_ge(stk_in[K_][c], group(nb, g, 32))
                        pe.wait_ge(stk_in[Q_][c], group(nb, g, 32))
                    n = CW if kc < c else max(2 * P, P * (r + 1))
                    nc.tensor.matmul(ring(o, u)[:, 0:n], qst[g % 2][0:KQ, c, h, P * r:P * r + P],
                                     kst[g % 2][0:KQ, kc, h, 0:n], start=True, stop=True).then_inc(ring_full, 1)
                elif kind == "M":
                    _, g, c = u
                    if c == 0:
                        pe.wait_ge(ring_free, used(o, b, maxima(g, 0)[-1]))
                    else:
                        pe.wait_ge(mcol_done, b * GROUPS + (g + 1))
                    nc.tensor.transpose(ring(o, u)[0:4 * QPC, 0:P], mst[:, 0, :] if c == 0 else mcol[:, :], ident[:, :])\
                        .then_inc(ring_full, 1)

            def scores(b, n, h):
                g, i = n // STEPS, n % STEPS
                c, kb, off = step_of(i)
                off = min(off, 2 * P)
                if h == 0 and kb == 0:
                    pe.wait_ge(mrow_in[c], group(b, g, 32))
                pe.wait_ge(s_exp, exps(b, 4 * n + h - 2))
                nc.tensor.matmul(sbank[h % 2][:, off:CW], kst[g % 2][0:KQ + 2, kb // QPC, h, P * (kb % QPC):P * (kb % QPC) + P],
                                 qst[g % 2][0:KQ + 2, c, h, off:CW], start=True, stop=True).then_inc(s_full, 1)

            def values(b, n):
                g, i = n // STEPS, n % STEPS
                c, kb, off = step_of(i)
                if kb == 0 and n:
                    pe.wait_ge(accv_free, evacuated(b, 2 * g + c - 1) - 1)
                if n == 0:
                    pe.wait_ge(ring_free, started(b))
                if diagonal(i):
                    pe.wait_ge(masked, b * NDIAG + (2 * QPC * g + i % QPC + (QPC if c else 0) + 1))
                else:
                    pe.wait_ge(s_exp, exps(b, 4 * n + 3))
                for h in range(4):
                    m = nc.tensor.matmul(accv[HD * h:HD * h + HD, off:CW], v[:, kb, P * g + HD * h:P * g + HD * h + HD],
                                     prob[:, n % 2, h, off:CW], start=(kb == 0), stop=(kb == QPC * (c + 1) - 1))
                m.then_inc(value_done, 1)

            def sums(b, n):
                g, i = n // STEPS, n % STEPS
                c, kb, off = step_of(i)
                if kb == 0 and n:
                    pe.wait_ge(acc_free, evacuated(b, 2 * g + c - 1))
                for h in range(4):
                    m = nc.tensor.matmul(accs[HD * h:HD * h + HD, off:CW], ones[:, 0:HD], prob[:, n % 2, h, off:CW],
                                         start=(kb == 0), stop=(kb == QPC * (c + 1) - 1))
                m.then_inc(step_used, 1)

            def sequence(o, b):
                for n in range(NSTEP):
                    g, i = n // STEPS, n % STEPS
                    first, second = filler(g, i)
                    if g == GROUPS - 1 and i >= STEPS - FIRST_SLOT:
                        first, second = o.slots[i - STEPS + FIRST_SLOT], []
                    scores(b, n, 0)
                    scores(b, n, 1)
                    for u in first:
                        use(o, b, u)
                    if g == GROUPS - 1 and i - 3 in EARLY:
                        output(o, b, ("O", i - 3), list(range(GROUPS - 1)))
                    if n:
                        values(b, n - 1)
                    scores(b, n, 2)
                    scores(b, n, 3)
                    for u in second:
                        use(o, b, u)
                    if n:
                        sums(b, n - 1)
                values(b, NSTEP - 1)
                sums(b, NSTEP - 1)
                for q in range(FIRST_SLOT, len(SLOTS)):
                    for u in o.slots[q]:
                        use(o, b, u)

            for q in range(FIRST_SLOT, len(SLOTS)):
                for u in HEAD.slots[q]:
                    use(HEAD, -1, u)
            with pe.Fori(0, B - 1) as b:
                sequence(BODY, b)
            sequence(TAIL, B - 1)


_INS = ["L0_attn_x", "L0_attn_Wqkv", "L0_attn_bqkv", "L0_attn_Wo", "L0_attn_bo", "L0_ffn_weight", "L0_ffn_bias"]
_OUTS = [((4, 1024, 512), "float32")]


def kernel(**inputs):
    import numpy as _np
    import concourse.bacc as _bacc
    from concourse import mybir as _mybir
    from concourse.bass_utils import run_bass_kernel_spmd as _run

    nc = _bacc.Bacc("TRN2", target_bir_lowering=False, num_devices=1)
    arrays, args = {}, []
    for name in _INS:
        a = _np.ascontiguousarray(inputs[name])
        arrays[f"in_{name}_dram"] = a
        args.append(nc.dram_tensor(f"in_{name}_dram", a.shape, _mybir.dt.from_np(a.dtype), kind="ExternalInput").ap())
    for i, (shape, dtype) in enumerate(_OUTS):
        dt = _mybir.dt.from_np(_np.dtype(dtype))
        args.append(nc.dram_tensor(f"out_{i}_dram", shape, dt, kind="ExternalOutput").ap())
    macaron_kernel(nc, *args)
    r = _run(nc, [arrays], core_ids=[0])
    got = tuple(r.results[0][f"out_{i}_dram"] for i in range(len(_OUTS)))
    return got[0]
```
